# Optimizing a Trainium2 kernel written in Bass

```python
import numpy as np
import jax
import jax.numpy as jnp

def _softmax(x, axis=-1):
    return jax.nn.softmax(x, axis=axis)

def _gelu(x):
    return jax.nn.gelu(x, approximate=True)

def _silu(x):
    return jax.nn.silu(x)

def _sigmoid(x):
    return jax.nn.sigmoid(x)

def _layernorm(x, axis=-1, eps=1e-05):
    m = jnp.mean(x, axis=axis, keepdims=True)
    v = jnp.var(x, axis=axis, keepdims=True)
    return (x - m) / jnp.sqrt(v + eps)

def _scatter_add(tgt, idx, src, axis=0):
    return tgt.at[idx].add(src)

def _segment_sum(src, seg, n):
    return jax.ops.segment_sum(src, seg, n)
kernel_name = 'mk_cond_seq_d2_seqx_r8_d147be'

def setup_inputs(seed: int=0):
    np.random.seed(seed)
    _w = jnp.asarray

    def _rec_inputs():
        import jax
        import jax.numpy as jnp
        _rk = jax.random.key(seed)
        x = -0.0003482 + 1 * jax.random.normal(jax.random.fold_in(_rk, 1), (8, 128, 144), jnp.float32)
        _lenS = 128 - jax.random.randint(jax.random.fold_in(_rk, 7), (8,), 0, max(1, 128 // 4) + 1, jnp.int32)
        _lenS2 = 128 - jax.random.randint(jax.random.fold_in(_rk, 8), (8,), 0, max(1, 128 // 4) + 1, jnp.int32)
        cond_1152 = 0.00257642 + 1.0011 * jax.random.normal(jax.random.fold_in(_rk, 11), (8, 144), jnp.float32)
        return (x, cond_1152)
    x, cond_1152 = _rec_inputs()

    def _L0_cond_setup():
        import jax, jax.numpy as jnp
        import numpy as np
        from jax.scipy.linalg import expm
        N, D, COND_DIM = (144, 64, 144)
        B, T = (16, 128)

        def _rotation(cond, W, b):
            v = jax.nn.silu(cond) @ W.T + b
            iu, ju = jnp.triu_indices(D, k=1)
            A = jnp.zeros((cond.shape[0], D, D), dtype=v.dtype)
            A = A.at[:, iu, ju].set(v).at[:, ju, iu].set(-v)
            return expm(A)
        key = jax.random.key(seed)
        k1, k2, k3, k4, k5 = jax.random.split(key, 5)
        x = jax.random.normal(k1, (B, T, N), dtype=jnp.float32)
        cond = jax.random.normal(k2, (B, COND_DIM), dtype=jnp.float32)
        P = jax.random.normal(k3, (N, D), dtype=jnp.float32)
        n_skew = D * (D - 1) // 2
        bound = 1.0 / np.sqrt(COND_DIM)
        W = jax.random.uniform(k4, (n_skew, COND_DIM), minval=-bound, maxval=bound, dtype=jnp.float32)
        b = jax.random.uniform(k5, (n_skew,), minval=-bound, maxval=bound, dtype=jnp.float32)
        return {'x': x, 'cond': cond, 'P': P, 'W': W, 'b': b}
    _L0_cond_all = _L0_cond_setup()
    _L0_cond_in = {k: v for k, v in _L0_cond_all.items() if k in ('P', 'W', 'b')}
    del _L0_cond_all

    def _L1_cond_setup():
        import jax, jax.numpy as jnp
        import numpy as np
        NUM_HEADS = 16
        NUM_EXPERTS = 4
        TOP_K = 2
        LN_EPS = 1e-06

        def _ln(h):
            mu = jnp.mean(h, axis=-1, keepdims=True)
            var = jnp.var(h, axis=-1, keepdims=True)
            return (h - mu) * jax.lax.rsqrt(var + LN_EPS)

        def _modulate(h, shift, scale):
            return h * (1.0 + scale[:, None, :]) + shift[:, None, :]
        key = jax.random.key(seed)
        ks = jax.random.split(key, 12)
        B, N, C = (8, 128, 144)
        H = 4 * C
        E = NUM_EXPERTS
        s = 0.02
        return {'x': jax.random.normal(ks[0], (B, N, C), jnp.float32), 'c': jax.random.normal(ks[1], (B, C), jnp.float32), 'w_adaln': jax.random.normal(ks[2], (C, 6 * C), jnp.float32) * s, 'b_adaln': jnp.zeros((6 * C,), jnp.float32), 'w_qkv': jax.random.normal(ks[3], (C, 3 * C), jnp.float32) * s, 'b_qkv': jnp.zeros((3 * C,), jnp.float32), 'w_proj': jax.random.normal(ks[4], (C, C), jnp.float32) * s, 'b_proj': jnp.zeros((C,), jnp.float32), 'w_gate': jax.random.normal(ks[5], (C, E), jnp.float32) * s, 'w1': jax.random.normal(ks[6], (E, C, H), jnp.float32) * s, 'b1': jnp.zeros((E, H), jnp.float32), 'w2': jax.random.normal(ks[7], (E, H, C), jnp.float32) * s, 'b2': jnp.zeros((E, C), jnp.float32)}
    _L1_cond_all = _L1_cond_setup()
    _L1_cond_in = {k: v for k, v in _L1_cond_all.items() if k in ('w_adaln', 'b_adaln', 'w_qkv', 'b_qkv', 'w_proj', 'b_proj', 'w_gate', 'w1', 'b1', 'w2', 'b2')}
    del _L1_cond_all
    return {'x': x, 'cond_1152': cond_1152, 'L0_cond_P': _L0_cond_in['P'], 'L0_cond_W': _L0_cond_in['W'], 'L0_cond_b': _L0_cond_in['b'], 'L1_cond_w_adaln': _L1_cond_in['w_adaln'], 'L1_cond_b_adaln': _L1_cond_in['b_adaln'], 'L1_cond_w_qkv': _L1_cond_in['w_qkv'], 'L1_cond_b_qkv': _L1_cond_in['b_qkv'], 'L1_cond_w_proj': _L1_cond_in['w_proj'], 'L1_cond_b_proj': _L1_cond_in['b_proj'], 'L1_cond_w_gate': _L1_cond_in['w_gate'], 'L1_cond_w1': _L1_cond_in['w1'], 'L1_cond_b1': _L1_cond_in['b1'], 'L1_cond_w2': _L1_cond_in['w2'], 'L1_cond_b2': _L1_cond_in['b2']}

def reference(x, cond_1152, L0_cond_P, L0_cond_W, L0_cond_b, L1_cond_w_adaln, L1_cond_b_adaln, L1_cond_w_qkv, L1_cond_b_qkv, L1_cond_w_proj, L1_cond_b_proj, L1_cond_w_gate, L1_cond_w1, L1_cond_b1, L1_cond_w2, L1_cond_b2):
    import jax
    import jax.numpy as jnp

    def _L0_cond_ref(x, cond, P, W, b):
        import jax, jax.numpy as jnp
        import numpy as np
        from jax.scipy.linalg import expm
        N, D, COND_DIM = (144, 64, 144)
        B, T = (16, 128)

        def _rotation(cond, W, b):
            v = jax.nn.silu(cond) @ W.T + b
            iu, ju = jnp.triu_indices(D, k=1)
            A = jnp.zeros((cond.shape[0], D, D), dtype=v.dtype)
            A = A.at[:, iu, ju].set(v).at[:, ju, iu].set(-v)
            return expm(A)
        U, _ = jnp.linalg.qr(P)
        R = _rotation(cond, W, b)
        z = jnp.einsum('btn,nd->btd', x, U)
        z_rot = jnp.einsum('btd,bde->bte', z, R)
        x_rot = x + jnp.einsum('btd,nd->btn', z_rot - z, U)
        return x_rot

    def _L1_cond_ref(x, c, w_adaln, b_adaln, w_qkv, b_qkv, w_proj, b_proj, w_gate, w1, b1, w2, b2):
        import jax, jax.numpy as jnp
        import numpy as np
        NUM_HEADS = 16
        NUM_EXPERTS = 4
        TOP_K = 2
        LN_EPS = 1e-06

        def _ln(h):
            mu = jnp.mean(h, axis=-1, keepdims=True)
            var = jnp.var(h, axis=-1, keepdims=True)
            return (h - mu) * jax.lax.rsqrt(var + LN_EPS)

        def _modulate(h, shift, scale):
            return h * (1.0 + scale[:, None, :]) + shift[:, None, :]
        B, N, C = x.shape
        nh = NUM_HEADS
        hd = C // nh
        mod = jax.nn.silu(c) @ w_adaln + b_adaln
        sh_msa, sc_msa, g_msa, sh_mlp, sc_mlp, g_mlp = jnp.split(mod, 6, axis=-1)
        h = _modulate(_ln(x), sh_msa, sc_msa)
        qkv = (h @ w_qkv + b_qkv).reshape(B, N, 3, nh, hd).transpose(2, 0, 3, 1, 4)
        q, k, v = (qkv[0], qkv[1], qkv[2])
        attn = jax.nn.softmax(jnp.einsum('bhqd,bhkd->bhqk', q, k) * hd ** (-0.5), axis=-1)
        o = jnp.einsum('bhqk,bhkd->bhqd', attn, v).transpose(0, 2, 1, 3).reshape(B, N, C)
        o = o @ w_proj + b_proj
        x = x + g_msa[:, None, :] * o
        xn = _modulate(_ln(x), sh_mlp, sc_mlp)
        xf = xn.reshape(-1, C)
        gate_logits = xf @ w_gate
        topk_logits, topk_idx = jax.lax.top_k(gate_logits, TOP_K)
        gates = jax.nn.softmax(topk_logits, axis=-1)
        cw = jnp.sum(jax.nn.one_hot(topk_idx, NUM_EXPERTS, dtype=xf.dtype) * gates[..., None], axis=1)
        hmid = jax.nn.gelu(jnp.einsum('tc,ech->eth', xf, w1) + b1[:, None, :], approximate=True)
        eo = jnp.einsum('eth,ehc->etc', hmid, w2) + b2[:, None, :]
        moe = jnp.einsum('te,etc->tc', cw, eo).reshape(B, N, C)
        return x + g_mlp[:, None, :] * moe
    x = _L0_cond_ref(x, cond_1152, L0_cond_P, L0_cond_W, L0_cond_b)
    x = _L1_cond_ref(x, cond_1152, L1_cond_w_adaln, L1_cond_b_adaln, L1_cond_w_qkv, L1_cond_b_qkv, L1_cond_w_proj, L1_cond_b_proj, L1_cond_w_gate, L1_cond_w1, L1_cond_b1, L1_cond_w2, L1_cond_b2)
    return x

_drawn_inputs = setup_inputs


def setup_inputs(seed=0):
    import zlib

    import numpy as np

    out = dict(_drawn_inputs(seed))
    spreads = {'L1_cond_b_adaln': (0.0, 0.555),
     'L1_cond_b_qkv': (0.0, 0.8),
     'L1_cond_b_proj': (0.0, 0.462),
     'L1_cond_b1': (0.0, 0.8),
     'L1_cond_b2': (0.0, 0.673)}
    factors = {'L1_cond_w_adaln': 3.062,
     'L1_cond_w_qkv': 8.0,
     'L1_cond_w_proj': 8.0,
     'L1_cond_w_gate': 5.929,
     'L1_cond_w1': 7.765,
     'L1_cond_w2': 7.198}
    for name, (base, spread) in spreads.items():
        noise = np.random.default_rng([zlib.crc32(name.encode()), seed]).standard_normal(out[name].shape)
        drawn = base * np.exp(spread * noise) if base else spread * noise
        out[name] = jnp.asarray(drawn.astype(out[name].dtype))
    for name, factor in factors.items():
        out[name] = (out[name] * factor).astype(out[name].dtype)
    return out
```

```python
from contextlib import ExitStack

import concourse.bass as bass
from concourse import mybir

ALU = mybir.AluOpType
ACT = mybir.ActivationFunctionType
F32 = mybir.dt.float32
I32 = mybir.dt.int32
AX_X = mybir.AxisListType.X
RMAX = bass.bass_isa.ReduceOp.max

P = 128
B, T, C = 8, 128, 144
D = 64
NH, HD = 16, 9
NE, HID = 4, 576
R = C - P
RA = R + 1
NSQ = 18
NTERM = 8
HEAD_SLOTS, STRIPS, STRIP = 4, 4, 32
VW = HD + 1
LN_EPS = 1e-6
QK_SCALE = float(HD) ** -0.5
HT5 = 5
HALF = 4 * T


def factorial(n):
    out = 1.0
    for i in range(2, n + 1):
        out *= i
    return out


def bass_conditional_rotation_moe_block(nc, xtok, xT, pmat, pT, condT, rotW, adaW, wq, wk, wv, wproj, wgate,
                                        w1, w2, b2, consts, out):
    with ExitStack() as ctx:
        def sb(name, shape, dt=F32):
            return ctx.enter_context(nc.sbuf_tensor(name, shape, dt))

        def sem(name):
            return ctx.enter_context(nc.semaphore(name))

        bank = [ctx.enter_context(nc.psum_tensor(f"bank{i}", [P, 512], F32)) for i in range(8)]

        cst = sb("cst", [P, consts.shape[1]])
        ident = cst[:, 0:P]
        id64 = cst[0:D, 0:D]
        half_id = cst[0:D, 128:192]
        below = cst[0:D, 192:256]
        skew_sign = cst[0:D, 256:320]
        thresholds = cst[0:D, 320:320 + NSQ]
        halvings = cst[0:D, 340:340 + NSQ]
        rank_ties = cst[:, 360:376]
        P_m, P_r = sb("P_m", [P, D]), sb("P_r", [R, D])
        PT = sb("PT", [D, C])
        xT_m, xT_r = sb("xT_m", [P, B * T]), sb("xT_r", [R, B * T])
        x_in = sb("x_in", [P, B, C])
        s_m, s_r = sb("s_m", [P, B]), sb("s_r", [RA, B])
        shared = sb("shared", [P, 3 * HEAD_SLOTS * B * T])
        part = [shared[:, i * 4096:(i + 1) * 4096] for i in range(3)]
        rot_m, rot_r = part[0], part[1][0:RA, :]
        ada_m, ada_r = sb("ada_m", [P, 6 * C]), sb("ada_r", [RA, 6 * C])
        wq_m, wq_r = sb("wq_m", [P, 512]), sb("wq_r", [RA, 512])
        wk_m, wk_r = sb("wk_m", [P, 512]), sb("wk_r", [RA, 512])
        wv_m, wv_r = sb("wv_m", [P, C]), sb("wv_r", [RA, C])
        wp_m, wp_r = sb("wp_m", [P, C]), sb("wp_r", [RA, C])
        wg_m, wg_r = sb("wg_m", [P, NE]), sb("wg_r", [R, NE])
        w1_m, w1_r = sb("w1_m", [P, NE * HID]), sb("w1_r", [RA, NE * HID])
        w2_m, w2_r = sb("w2_m", [P, NE, 4, C]), sb("w2_r", [HID - 512, NE, C])
        b2_s = sb("b2_s", [NE, C])

        EL = sb("EL", [D, 2 * D])
        rpiv, coef = sb("rpiv", [D, 1]), sb("coef", [D, 1])
        piv, rnorm = sb("piv", [D, 1]), sb("rnorm", [D, 1])
        mhalf = sb("mhalf", [P, B])
        LT = sb("LT", [D, D])
        xPT = sb("xPT", [D, B * T])
        U0T = sb("U0T", [D, C])
        Z0T = sb("Z0T", [D, B * T])
        Y = sb("Y", [D, D])
        SG = sb("SG", [D, D])
        den, rden, dcoef = sb("den", [D, 1]), sb("rden", [D, 1]), sb("dcoef", [D, 1])
        tmp64 = sb("tmp64", [D, D])
        sigma = sb("sigma", [D, 1])

        A = sb("A", [D, B, D])
        norms, norm = sb("norms", [D, B]), sb("norm", [D, B])
        active = sb("active", [D, NSQ, B])
        shrink, scale = sb("shrink", [D, B, NSQ]), sb("scale", [D, B])
        Npow = [sb(f"Npow{i}", [D, B, D]) for i in range(1, 5)]
        poly = {n: sb(n, [D, B, D]) for n in ("Chi", "Dhi", "Clo", "Dlo")}
        E = [sb("E0", [D, B, D]), sb("E1", [D, B, D])]
        WT = sb("WT", [D, B * T])

        MOD_m, MOD_r = sb("MOD_m", [P, 4, B]), sb("MOD_r", [R, 4, B])
        GB = sb("GB", [P, B, 2, C])
        XR = sb("XR", [P, B, C])
        stats = sb("stats", [P, B, 6])
        mv = sb("mv", [P, B, 2])
        veps, rstd = sb("veps", [P, B]), sb("rstd", [P, B])
        H = sb("H", [P, B, C])
        HT_m, HT_r = sb("HT_m", [P, B * T]), sb("HT_r", [RA, B * T])
        QT = part[0].rearrange("p (t n) -> p t n", t=HEAD_SLOTS)
        KT = part[1].rearrange("p (t n) -> p t n", t=HEAD_SLOTS)
        VA = sb("VA", [P, B, NH, VW])
        NM = sb("NM", [P, 2, HEAD_SLOTS, P])
        PR = part[2].rearrange("p (s h q) -> p s h q", s=2, h=NH)
        rsum = sb("rsum", [P, 2, NH])
        OA = sb("OA", [P, 2, C])
        OT_m, OT_r = sb("OT_m", [P, 2, T]), sb("OT_r", [RA, 2, T])
        PG = sb("PG", [P, 2, C])
        X2 = sb("X2", [P, B, C])
        lg = sb("lg", [P, B, NE])
        gt, eq = sb("gt", [P, B, NE, NE]), sb("eq", [P, B, NE, NE])
        rank = sb("rank", [P, B, NE])
        gmax = sb("gmax", [P, B])
        gsum, rgs = sb("gsum", [P, B]), sb("rgs", [P, B])
        sel = sb("sel", [P, B, NE])
        cw = sb("cw", [P, B, NE])
        cwT = sb("cwT", [NE, B * T])
        HM = shared[:, 0:NE * HT5 * HALF].rearrange("p (j n) -> p j n", j=NE * HT5)
        ACC = sb("ACC", [P, 2, C])
        RES = sb("RES", [P, B, C])

        in_cst, in_qr, in_cond, in_rot, in_x, in_ada, in_attn, in_moe = (sem(n) for n in (
            "in_cst", "in_qr", "in_cond", "in_rot", "in_x", "in_ada", "in_attn", "in_moe"))
        dve_done = sem("dve_done")
        pool_done = sem("pool_done")
        silu_done = sem("silu_done")
        names = ("gram_ready row_ready row_used linv_ready linvT_ready lT_ready basis_ready yrow_ready yrow_used "
                 "a_ready ent_ready norms_ready norm_ready npow_mm npow_sb poly_sb hi_mm cd_ready ad_mm e_ready sq_mm "
                 "piv_ready rnorm_ready xp_ready xp_sb z_ready turn_ready turned_ready wt_ready delta_ready ones_set "
                 "f_ready xr_used var_ready rstd_ready h_ready hT_mm hT_sb mod_mm mod_sb gate_mm gate_sb "
                 "proj_mm q_sb v_sb scoreA mx_ready mxT_mm qm_ready scoreB pr_ready pv_mm o_ready oT_mm oT_sb "
                 "attn_mm x2_ready lg_mm lg_sb cw_ready cwT_mm cwT_sb up_mm act_ready down_mm down_used "
                 "res_ready stored nm_zero").split()
        S = {n: sem(n) for n in names}

        block = ctx.enter_context(nc.Block())

        def rt(ap, b):
            return ap[:, b * T:(b + 1) * T]

        @block.sync
        def _(sp):
            sp.dma_start(cst[:], consts).then_inc(in_cst, 16)
            sp.dma_start(P_m[:], pmat[0:P, :]).then_inc(in_qr, 16)
            sp.dma_start(P_r[:], pmat[P:C, :]).then_inc(in_qr, 16)
            sp.dma_start(s_m[:], condT[0:P, :]).then_inc(in_cond, 16)
            sp.dma_start(s_r[:], condT[P:C + 1, :]).then_inc(in_cond, 16)
            sp.dma_start(rot_m, rotW[0:P, :]).then_inc(in_rot, 16)
            sp.dma_start(rot_r, rotW[P:C + 1, :]).then_inc(in_rot, 16)
            sp.dma_start(PT[:], pT).then_inc(in_x, 16)
            sp.dma_start(xT_m[:], xT[0:P, :]).then_inc(in_x, 16)
            sp.dma_start(xT_r[:], xT[P:C, :]).then_inc(in_x, 16)
            sp.dma_start(x_in[:], xtok.rearrange("b t c -> t b c")).then_inc(in_x, 16)
            sp.dma_start(ada_m[:], adaW[0:P, :]).then_inc(in_ada, 16)
            sp.dma_start(ada_r[:], adaW[P:C + 1, :]).then_inc(in_ada, 16)
            for m, r, w in ((wq_m, wq_r, wq), (wk_m, wk_r, wk), (wv_m, wv_r, wv), (wp_m, wp_r, wproj)):
                sp.dma_start(m[:], w[0:P, :]).then_inc(in_attn, 16)
                sp.dma_start(r[:], w[P:C + 1, :]).then_inc(in_attn, 16)
            sp.dma_start(wg_m[:], wgate[0:P, :]).then_inc(in_moe, 16)
            sp.dma_start(wg_r[:], wgate[P:C, :]).then_inc(in_moe, 16)
            sp.dma_start(w1_m[:], w1[0:P, :]).then_inc(in_moe, 16)
            sp.dma_start(w1_r[:], w1[P:C + 1, :]).then_inc(in_moe, 16)
            for e in range(NE):
                sp.dma_start(w2_m[:, e, :, :],
                             w2[e, 0:512, :].rearrange("(t p) c -> p t c", p=P)).then_inc(in_moe, 16)
            sp.dma_start(w2_r[:], w2[:, 512:HID, :].rearrange("e p c -> p e c")).then_inc(in_moe, 16)
            sp.dma_start(b2_s[:], b2).then_inc(in_moe, 16)
            for b in range(B):
                sp.wait_ge(S["res_ready"], b + 1)
                sp.dma_start(out[b], RES[:, b, :]).then_inc(S["stored"], 16)
            sp.wait_ge(S["stored"], 16 * B)
        N_MOE = 16 * 10

        @block.gpsimd
        def _(pool):
            nc.gpsimd.memset(mhalf[:], -0.5).then_inc(pool_done, 1)
            nc.gpsimd.memset(HT_r[:], 1.0).then_inc(S["ones_set"], 1)
            nc.gpsimd.memset(OT_r[:], 1.0).then_inc(S["ones_set"], 1)
            nc.gpsimd.memset(VA[:], 1.0).then_inc(S["ones_set"], 1)
            nc.gpsimd.memset(NM[:], 0.0).then_inc(S["nm_zero"], 1)
            pool.wait_ge(S["norms_ready"], 1)
            nc.gpsimd.partition_all_reduce(norm[:], norms[:], D, RMAX).then_inc(S["norm_ready"], 1)
            pool.wait_ge(S["piv_ready"], 1)
            pool.wait_ge(pool_done, 1)
            nc.gpsimd.tensor_tensor(rnorm[:], piv[:], mhalf[0:D, 0:1], ALU.pow).then_inc(S["rnorm_ready"], 1)
            for ln in range(2):
                pool.wait_ge(S["var_ready"], B * (ln + 1))
                nc.gpsimd.tensor_scalar(veps[:], mv[:, :, 1], LN_EPS, None, ALU.add).then_inc(pool_done, 1)
                pool.wait_ge(pool_done, ln + 2)
                nc.gpsimd.tensor_tensor(rstd[:], veps[:], mhalf[:], ALU.pow).then_inc(S["rstd_ready"], 1)

        @block.scalar
        def _(act):
            act.wait_ge(in_cond, 32)
            nc.scalar.activation(s_m[:], s_m[:], ACT.Silu).then_inc(silu_done, 1)
            nc.scalar.activation(s_r[0:R, :], s_r[0:R, :], ACT.Silu).then_inc(silu_done, 1)
            for i in range(4):
                act.wait_ge(S["npow_mm"], i + 1)
                nc.scalar.activation(Npow[i][:], bank[3 + i % 2][0:D, :].rearrange("p (b j) -> p b j", b=B),
                                     ACT.Copy).then_inc(S["npow_sb"], 1)
            for b in range(B):
                act.wait_ge(S["gate_mm"], b + 1)
                nc.scalar.activation(GB[:, b, :, :], bank[6 + b % 2][:, 0:2 * C].rearrange("p (g c) -> p g c", g=2),
                                     ACT.Copy).then_inc(S["gate_sb"], 1)
            for h in range(2):
                act.wait_ge(S["xp_ready"], h + 1)
                nc.scalar.activation(xPT[:, h * 512:(h + 1) * 512], bank[6 + h][0:D, :], ACT.Copy)\
                    .then_inc(S["xp_sb"], 1)

            def modulated(ln):
                for b in range(B):
                    act.wait_ge(S["hT_mm"], ln * B + b + 1)
                    src = bank[4 + b % 2]
                    nc.scalar.activation(rt(HT_m, b), src[:, 0:T], ACT.Identity, bias=MOD_m[:, 2 * ln, b:b + 1],
                                         scale=MOD_m[:, 2 * ln + 1, b:b + 1])
                    nc.scalar.activation(rt(HT_r, b)[0:R, :], src[0:R, T:2 * T], ACT.Identity,
                                         bias=MOD_r[:, 2 * ln, b:b + 1],
                                         scale=MOD_r[:, 2 * ln + 1, b:b + 1]).then_inc(S["hT_sb"], 1)

            act.wait_ge(S["ones_set"], 3)
            act.wait_ge(S["mod_sb"], 1)
            modulated(0)
            n = 0
            for h in range(2):
                for dst in (QT, KT):
                    for t in range(HEAD_SLOTS):
                        act.wait_ge(S["proj_mm"], n + 1)
                        nc.scalar.activation(dst[:, t, h * 512:(h + 1) * 512], bank[n % 2][:, :], ACT.Copy)\
                            .then_inc(S["q_sb"], 1)
                        n += 1
            for b in range(B):
                for t in range(HEAD_SLOTS):
                    act.wait_ge(S["scoreB"], b * 4 + t + 1)
                    if b >= 2 and t == 0:
                        act.wait_ge(S["pv_mm"], b - 1)
                    nc.scalar.activation(PR[:, b % 2, 4 * t:4 * t + 4, :],
                                         bank[2 + t % 2][:, :].rearrange("p (h q) -> p h q", h=4),
                                         ACT.Exp, scale=QK_SCALE).then_inc(S["pr_ready"], 1)
                act.wait_ge(S["oT_mm"], b + 1)
                if b >= 2:
                    act.wait_ge(S["attn_mm"], b - 1)
                nc.scalar.activation(OT_m[:, b % 2, :], bank[6][:, 0:T], ACT.Copy)
                nc.scalar.activation(OT_r[0:R, b % 2, :], bank[6][0:R, T:2 * T], ACT.Copy).then_inc(S["oT_sb"], 1)
            modulated(1)
            act.wait_ge(S["lg_mm"], 1)
            nc.scalar.activation(lg[:], bank[6][:, 0:B * NE].rearrange("p (b e) -> p b e", b=B), ACT.Copy)\
                .then_inc(S["lg_sb"], 1)
            act.wait_ge(S["x2_ready"], B + 1)
            nc.scalar.activation(sel[:], sel[:], ACT.Exp).then_inc(S["lg_sb"], 1)
            for h in range(2):
                act.wait_ge(S["cwT_mm"], h + 1)
                nc.scalar.activation(cwT[:, h * 512:(h + 1) * 512], bank[6 + h][0:NE, :], ACT.Copy)\
                    .then_inc(S["cwT_sb"], 1)
            n = 0
            for h in range(2):
                for j in range(NE * HT5):
                    rows = P if j % HT5 < 4 else HID - 512
                    act.wait_ge(S["up_mm"], n + 1)
                    if h:
                        act.wait_ge(S["down_mm"], 8)
                    nc.scalar.activation(HM[0:rows, j, :], bank[n % 3][0:rows, :], ACT.Gelu_apprx_tanh)\
                        .then_inc(S["act_ready"], 1)
                    n += 1

        @block.tensor
        def _(pe):
            mm = nc.tensor.matmul
            pe.wait_ge(in_qr, 32)
            mm(bank[0][0:D, 0:D], P_m[:], P_m[:], start=True, stop=False)
            mm(bank[0][0:D, 0:D], P_r[:], P_r[:], start=False, stop=True).then_inc(S["gram_ready"], 1)
            pe.wait_ge(in_rot, 32)
            pe.wait_ge(silu_done, 2)
            for j in range(D):
                dst = bank[2][0:D, j * B:(j + 1) * B]
                mm(dst, rot_m[:, j * D:(j + 1) * D], s_m[:], start=True, stop=False)
                last = mm(dst, rot_r[:, j * D:(j + 1) * D], s_r[:], start=False, stop=True)
            last.then_inc(S["ent_ready"], 1)

            def each(dst, left, right):
                for b in range(B):
                    last = mm(dst[0:D, b * D:(b + 1) * D], left[:, b, :], right[:, b, :], start=True, stop=True)
                return last

            pe.wait_ge(S["a_ready"], 1)
            each(bank[3], A, A).then_inc(S["npow_mm"], 1)
            pe.wait_ge(S["npow_sb"], 1)
            each(bank[4], Npow[0], Npow[0]).then_inc(S["npow_mm"], 1)
            pe.wait_ge(S["npow_sb"], 2)
            each(bank[3], Npow[0], Npow[1]).then_inc(S["npow_mm"], 1)
            pe.wait_ge(S["npow_sb"], 3)
            each(bank[4], Npow[1], Npow[1]).then_inc(S["npow_mm"], 1)
            pe.wait_ge(S["npow_sb"], 4)
            pe.wait_ge(S["poly_sb"], 1)
            each(bank[5], Npow[3], poly["Chi"])
            each(bank[6], Npow[3], poly["Dhi"]).then_inc(S["hi_mm"], 1)
            pe.wait_ge(S["cd_ready"], 1)
            each(bank[7], A, poly["Dlo"]).then_inc(S["ad_mm"], 1)
            for k in range(NSQ):
                pe.wait_ge(S["e_ready"], k + 1)
                each(bank[3], E[1], E[0])
                each(bank[4], E[0], E[1]).then_inc(S["sq_mm"], 1)
            pe.wait_ge(in_ada, 32)
            for n, ch in enumerate((0, 1, 3, 4)):
                dst = bank[5][:, n * B:(n + 1) * B]
                mm(dst, ada_m[:, ch * C:ch * C + P], s_m[:], start=True, stop=False)
                mm(dst, ada_r[:, ch * C:ch * C + P], s_r[:], start=False, stop=True)
            for n, ch in enumerate((0, 1, 3, 4)):
                dst = bank[5][0:R, 64 + n * B:64 + (n + 1) * B]
                mm(dst, ada_m[:, ch * C + P:(ch + 1) * C], s_m[:], start=True, stop=False)
                last = mm(dst, ada_r[:, ch * C + P:(ch + 1) * C], s_r[:], start=False, stop=True)
            last.then_inc(S["mod_mm"], 1)
            gm = ada_m[:].rearrange("p (g k c) -> p g k c", g=2, k=3)[:, :, 2, :]
            gr = ada_r[:].rearrange("p (g k c) -> p g k c", g=2, k=3)[:, :, 2, :]
            for b in range(B):
                if b >= 2:
                    pe.wait_ge(S["gate_sb"], b - 1)
                else:
                    pe.wait_ge(S["cd_ready"], 1)
                dst = bank[6 + b % 2][:, 0:2 * C]
                mm(dst, s_m[:, b:b + 1].to_broadcast([P, P]), gm, start=True, stop=False)
                mm(dst, s_r[:, b:b + 1].to_broadcast([RA, P]), gr, start=False, stop=True)\
                    .then_inc(S["gate_mm"], 1)
            pe.wait_ge(in_x, 64)
            for h in range(2):
                pe.wait_ge(S["gate_sb"], B - 1 + h)
                dst = bank[6 + h][0:D, :]
                mm(dst, P_m[:], xT_m[:, h * 512:(h + 1) * 512], start=True, stop=False)
                mm(dst, P_r[:], xT_r[:, h * 512:(h + 1) * 512], start=False, stop=True)\
                    .then_inc(S["xp_ready"], 1)

            for k in range(D - 1):
                pe.wait_ge(S["row_used"], k + 1)
                mm(bank[k % 2][0:D, 0:D + 1], ident[0:D, k:k + 1].to_broadcast([D, D]), EL[:, k:k + D + 1],
                   start=True, stop=True).then_inc(S["row_ready"], 1)
            pe.wait_ge(S["row_used"], D)
            nc.tensor.transpose(bank[0][0:D, 0:D], EL[:, D:2 * D], id64).then_inc(S["linvT_ready"], 1)
            pe.wait_ge(S["lT_ready"], 1)
            mm(bank[1][0:D, 0:C], LT[:], PT[:], start=True, stop=True).then_inc(S["basis_ready"], 1)
            pe.wait_ge(S["xp_sb"], 2)
            for h in range(2):
                mm(bank[2 + h][0:D, :], LT[:], xPT[:, h * 512:(h + 1) * 512], start=True, stop=True)\
                    .then_inc(S["z_ready"], 1)
            for k in range(D):
                pe.wait_ge(S["yrow_used"], k + 1)
                mm(bank[k % 2][0:D, 0:D - k], ident[0:D, k:k + 1].to_broadcast([D, D]), Y[:, k:D],
                   start=True, stop=True).then_inc(S["yrow_ready"], 1)
            pe.wait_ge(S["f_ready"], 1)
            for b in range(B):
                last = mm(bank[4 + b // 4][0:D, (b % 4) * T:(b % 4 + 1) * T], E[0][:, b, :], rt(Z0T, b),
                          start=True, stop=True)
                if b % 4 == 3:
                    last.then_inc(S["turn_ready"], 1)
            for b in range(B):
                pe.wait_ge(S["turned_ready"], b // 4 + 1)
                if b >= 2:
                    pe.wait_ge(S["xr_used"], b - 1)
                mm(bank[b % 2][:, 0:C], rt(WT, b), U0T[:], start=True, stop=True).then_inc(S["delta_ready"], 1)

            def transposed(ln):
                for b in range(B):
                    pe.wait_ge(S["h_ready"], ln * B + b + 1)
                    if b >= 2:
                        pe.wait_ge(S["hT_sb"], ln * B + b - 1)
                    nc.tensor.transpose(bank[4 + b % 2][:, 0:T], H[:, b, 0:P], ident)
                    nc.tensor.transpose(bank[4 + b % 2][0:R, T:2 * T], H[:, b, P:C], ident)\
                        .then_inc(S["hT_mm"], 1)

            transposed(0)
            pe.wait_ge(in_attn, 128)
            n = 0
            for h in range(2):
                pe.wait_ge(S["hT_sb"], 4 * h + 4)
                for wm, wr in ((wq_m, wq_r), (wk_m, wk_r)):
                    for t in range(HEAD_SLOTS):
                        if n >= 2:
                            pe.wait_ge(S["q_sb"], n - 1)
                        dst = bank[n % 2][:, :]
                        mm(dst, wm[:, t * P:(t + 1) * P], HT_m[:, h * 512:(h + 1) * 512], start=True, stop=False)
                        mm(dst, wr[:, t * P:(t + 1) * P], HT_r[:, h * 512:(h + 1) * 512], start=False, stop=True)\
                            .then_inc(S["proj_mm"], 1)
                        n += 1
            for b in range(B):
                if b >= 2:
                    pe.wait_ge(S["v_sb"], b - 1)
                dst = bank[2 + b % 2][:, 0:C]
                mm(dst, rt(HT_m, b), wv_m[:], start=True, stop=False)
                mm(dst, rt(HT_r, b), wv_r[:], start=False, stop=True).then_inc(S["proj_mm"], 1)

            pe.wait_ge(S["q_sb"], 16)
            pe.wait_ge(S["v_sb"], B)

            def scores_a(b):
                for s in range(STRIPS):
                    i = b * 4 + s
                    if i >= 2:
                        pe.wait_ge(S["mx_ready"], i - 1)
                    for t in range(HEAD_SLOTS):
                        r = slice(s * STRIP, s * STRIP + HD)
                        last = mm(bank[s % 2][:, t * T:(t + 1) * T], QT[r, t, b * T:(b + 1) * T],
                                  KT[r, t, b * T:(b + 1) * T], start=True, stop=True)
                    last.then_inc(S["scoreA"], 1)

            def rest(b):
                pe.wait_ge(S["mx_ready"], 4 * b + 4)
                for t in range(HEAD_SLOTS):
                    last = nc.tensor.transpose(bank[4][:, t * T:(t + 1) * T], NM[:, b % 2, t, :], ident)
                last.then_inc(S["mxT_mm"], 1)
                pe.wait_ge(S["qm_ready"], b + 1)
                for s in range(STRIPS):
                    i = b * 4 + s
                    if i >= 2:
                        pe.wait_ge(S["pr_ready"], i - 1)
                    for t in range(HEAD_SLOTS):
                        r = slice(s * STRIP, s * STRIP + HD + 1)
                        last = mm(bank[2 + s % 2][:, t * T:(t + 1) * T], KT[r, t, b * T:(b + 1) * T],
                                  QT[r, t, b * T:(b + 1) * T], start=True, stop=True)
                    last.then_inc(S["scoreB"], 1)
                pe.wait_ge(S["pr_ready"], 4 * b + 4)
                if b >= 1:
                    pe.wait_ge(S["o_ready"], b)
                for h in range(NH):
                    last = mm(bank[5][:, h * VW:(h + 1) * VW], PR[:, b % 2, h, :], VA[:, b, h, :],
                              start=True, stop=True)
                last.then_inc(S["pv_mm"], 1)
                pe.wait_ge(S["o_ready"], b + 1)
                if b >= 1:
                    pe.wait_ge(S["oT_sb"], b)
                nc.tensor.transpose(bank[6][:, 0:T], OA[:, b % 2, 0:P], ident)
                nc.tensor.transpose(bank[6][0:R, T:2 * T], OA[:, b % 2, P:C], ident).then_inc(S["oT_mm"], 1)
                pe.wait_ge(S["oT_sb"], b + 1)
                if b >= 1:
                    pe.wait_ge(S["x2_ready"], b)
                mm(bank[7][:, 0:C], OT_m[:, b % 2, :], wp_m[:], start=True, stop=False)
                mm(bank[7][:, 0:C], OT_r[:, b % 2, :], wp_r[:], start=False, stop=True).then_inc(S["attn_mm"], 1)

            scores_a(0)
            for b in range(B):
                if b + 1 < B:
                    scores_a(b + 1)
                rest(b)

            transposed(1)
            pe.wait_ge(in_moe, N_MOE)
            pe.wait_ge(S["hT_sb"], 2 * B)
            for b in range(B):
                dst = bank[6][:, b * NE:(b + 1) * NE]
                mm(dst, rt(HT_m, b), wg_m[:], start=True, stop=False)
                last = mm(dst, rt(HT_r, b)[0:R, :], wg_r[:], start=False, stop=True)
            last.then_inc(S["lg_mm"], 1)
            pe.wait_ge(S["cw_ready"], 1)
            for h in range(2):
                for b in range(4 * h, 4 * h + 4):
                    last = nc.tensor.transpose(bank[6 + h][0:NE, (b % 4) * T:(b % 4 + 1) * T], cw[:, b, :], ident)
                last.then_inc(S["cwT_mm"], 1)

            n = 0
            for h in range(2):
                for j in range(NE * HT5):
                    e, t = divmod(j, HT5)
                    rows = P if t < 4 else HID - 512
                    cols = slice(e * HID + t * P, e * HID + t * P + rows)
                    if n >= 3:
                        pe.wait_ge(S["act_ready"], n - 2)
                    dst = bank[n % 3][0:rows, :]
                    mm(dst, w1_m[:, cols], HT_m[:, h * 512:(h + 1) * 512], start=True, stop=False)
                    mm(dst, w1_r[:, cols], HT_r[:, h * 512:(h + 1) * 512], start=False, stop=True)\
                        .then_inc(S["up_mm"], 1)
                    n += 1
                pe.wait_ge(S["act_ready"], 20 * h + 20)
                pe.wait_ge(S["cwT_sb"], 2)
                for b in range(4 * h, 4 * h + 4):
                    i = b % 4
                    if b >= 1:
                        pe.wait_ge(S["down_used"], b)
                    mm(bank[5][:, 0:C], rt(cwT, b), b2_s[:], start=True, stop=True)
                    for pair in range(2):
                        for e in (2 * pair, 2 * pair + 1):
                            dst = bank[3 + pair][:, (e % 2) * C:(e % 2 + 1) * C]
                            for t in range(4):
                                mm(dst, HM[:, e * HT5 + t, i * T:(i + 1) * T], w2_m[:, e, t, :],
                                   start=(t == 0), stop=False)
                            last = mm(dst, HM[0:HID - 512, e * HT5 + 4, i * T:(i + 1) * T], w2_r[:, e, :],
                                      start=False, stop=True)
                        last.then_inc(S["down_mm"], 1)

        count = [0]

        @block.vector
        def _(dve):
            V = nc.vector

            def seq(ins):
                count[0] += 1
                ins.then_inc(dve_done, 1)
                dve.wait_ge(dve_done, count[0])

            dve.wait_ge(in_cst, 16)
            dve.wait_ge(S["ent_ready"], 1)
            seq(V.tensor_tensor(A[:], bank[2][0:D, :].rearrange("p (j b) -> p b j", b=B),
                                skew_sign.unsqueeze(1).to_broadcast([D, B, D]), ALU.mult))
            V.tensor_reduce(norms[:], A[:], AX_X, ALU.add, apply_absolute_value=True).then_inc(S["norms_ready"], 1)
            dve.wait_ge(S["norm_ready"], 1)
            seq(V.tensor_tensor(active[:], norm[:].unsqueeze(1).to_broadcast([D, NSQ, B]),
                                thresholds.unsqueeze(2).to_broadcast([D, NSQ, B]), ALU.is_gt))
            seq(V.tensor_tensor(shrink[:], active[:].rearrange("p k b -> p b k"),
                                halvings.unsqueeze(1).to_broadcast([D, B, NSQ]), ALU.mult))
            seq(V.tensor_reduce(scale[:], shrink[:], AX_X, ALU.add))
            seq(V.tensor_scalar(scale[:], scale[:], -1.0, 1.0, ALU.mult, ALU.add))
            V.tensor_tensor(A[:], A[:], scale[:].unsqueeze(2).to_broadcast([D, B, D]), ALU.mult)\
                .then_inc(S["a_ready"], 1)
            idb = id64.unsqueeze(1).to_broadcast([D, B, D])
            cosc = [(-1.0) ** i / factorial(2 * i) for i in range(NTERM)]
            sinc = [(-1.0) ** i / factorial(2 * i + 1) for i in range(NTERM)]
            dve.wait_ge(S["npow_sb"], 3)
            for name, c in (("Chi", cosc[4:]), ("Dhi", sinc[4:]), ("Clo", cosc[:4]), ("Dlo", sinc[:4])):
                p = poly[name]
                seq(V.tensor_scalar(p[:], Npow[2][:], c[3], None, ALU.mult))
                seq(V.scalar_tensor_tensor(p[:], Npow[1][:], c[2], p[:], ALU.mult, ALU.add))
                seq(V.scalar_tensor_tensor(p[:], Npow[0][:], c[1], p[:], ALU.mult, ALU.add))
                ins = V.scalar_tensor_tensor(p[:], idb, c[0], p[:], ALU.mult, ALU.add)
                seq(ins)
                if name == "Dhi":
                    V.tensor_copy(coef[:], scale[:, 0:1]).then_inc(S["poly_sb"], 1)
            dve.wait_ge(S["hi_mm"], 1)

            def psb(n):
                return bank[n][0:D, :].rearrange("p (b j) -> p b j", b=B)

            seq(V.tensor_tensor(poly["Dlo"][:], psb(6), poly["Dlo"][:], ALU.add))
            V.tensor_tensor(poly["Clo"][:], psb(5), poly["Clo"][:], ALU.add).then_inc(S["cd_ready"], 1)
            dve.wait_ge(S["ad_mm"], 1)
            dve.wait_ge(S["cd_ready"], 1)
            seq(V.tensor_tensor(E[1][:], psb(7), poly["Clo"][:], ALU.add))
            V.scalar_tensor_tensor(E[0][:], psb(7), -1.0, poly["Clo"][:], ALU.mult, ALU.add)\
                .then_inc(S["e_ready"], 1)
            for k in range(NSQ):
                dve.wait_ge(S["sq_mm"], k + 1)
                dve.wait_ge(S["e_ready"], k + 1)
                mask = active[:, k, :].unsqueeze(2).to_broadcast([D, B, D]).bitcast(I32)
                seq(V.copy_predicated(E[0][:], mask, psb(3)))
                V.copy_predicated(E[1][:], mask, psb(4)).then_inc(S["e_ready"], 1)
            dve.wait_ge(S["e_ready"], NSQ + 1)
            seq(V.tensor_tensor(E[0][:], E[0][:], idb, ALU.subtract))

            dve.wait_ge(S["mod_mm"], 1)
            seq(V.tensor_copy(MOD_m[:], bank[5][:, 0:4 * B].rearrange("p (c b) -> p c b", c=4)))
            seq(V.tensor_copy(MOD_r[:], bank[5][0:R, 64:64 + 4 * B].rearrange("p (c b) -> p c b", c=4)))
            for m in (MOD_m, MOD_r):
                sc = m[:].rearrange("p (l k) b -> p l k b", l=2)[:, :, 1, :]
                ins = V.tensor_scalar(sc, sc, 1.0, None, ALU.add)
                seq(ins)
            V.tensor_copy(coef[:], scale[:, 0:1]).then_inc(S["mod_sb"], 1)
            dve.wait_ge(S["mod_sb"], 1)

            dve.wait_ge(S["gram_ready"], 1)
            seq(V.tensor_copy(EL[:, 0:D], bank[0][0:D, 0:D]))
            V.tensor_copy(EL[:, D:2 * D], id64).then_inc(S["row_used"], 1)
            for k in range(D - 1):
                row = bank[k % 2]
                dve.wait_ge(S["row_ready"], k + 1)
                seq(V.reciprocal(rpiv[:], row[0:D, 0:1]))
                seq(V.tensor_scalar(coef[:], EL[:, k:k + 1], rpiv[:], below[:, k:k + 1], ALU.mult, ALU.mult))
                win = EL[:, k + 1:k + 1 + D]
                V.scalar_tensor_tensor(win, row[0:D, 1:D + 1], coef[:], win, ALU.mult, ALU.add)\
                    .then_inc(S["row_used"], 1)
                dve.wait_ge(S["row_used"], k + 2)
            seq(V.tensor_tensor(tmp64[:], EL[:, 0:D], id64, ALU.mult))
            V.tensor_reduce(piv[:], tmp64[:], AX_X, ALU.add).then_inc(S["piv_ready"], 1)
            dve.wait_ge(S["linvT_ready"], 1)
            V.tensor_copy(LT[:], bank[0][0:D, 0:D]).then_inc(S["lT_ready"], 1)
            dve.wait_ge(S["rnorm_ready"], 1)
            dve.wait_ge(S["basis_ready"], 1)
            seq(V.tensor_scalar(U0T[:], bank[1][0:D, 0:C], rnorm[:], None, ALU.mult))
            V.scalar_tensor_tensor(Y[:], U0T[:, 0:D], 0.5, half_id, ALU.mult, ALU.subtract)\
                .then_inc(S["yrow_used"], 1)
            dve.wait_ge(S["z_ready"], 2)
            for h in range(2):
                seq(V.tensor_scalar(Z0T[:, h * 512:(h + 1) * 512], bank[2 + h][0:D, :], rnorm[:], None, ALU.mult))
            dve.wait_ge(S["yrow_used"], 1)
            for k in range(D):
                row = bank[k % 2]
                dve.wait_ge(S["yrow_ready"], k + 1)
                seq(V.tensor_scalar(den[:], row[0:D, 0:1], -0.5, row[0:D, 0:1], ALU.is_ge, ALU.add))
                seq(V.tensor_scalar(SG[:, k:k + 1], row[0:D, 0:1], -0.5, None, ALU.is_ge))
                if k == D - 1:
                    break
                seq(V.reciprocal(rden[:], den[:]))
                seq(V.tensor_scalar(dcoef[:], Y[:, k:k + 1], rden[:], -1.0, ALU.mult, ALU.mult))
                V.scalar_tensor_tensor(Y[:, k + 1:D], row[0:D, 1:D - k], dcoef[:], Y[:, k + 1:D],
                                       ALU.mult, ALU.add).then_inc(S["yrow_used"], 1)
                dve.wait_ge(S["yrow_used"], k + 2)
            seq(V.tensor_tensor(tmp64[:], SG[:], id64, ALU.mult))
            seq(V.tensor_reduce(sigma[:], tmp64[:], AX_X, ALU.add))
            seq(V.tensor_scalar(sigma[:], sigma[:], 2.0, -1.0, ALU.mult, ALU.add))
            V.tensor_scalar(E[0][:], E[0][:], sigma[:], None, ALU.mult).then_inc(S["f_ready"], 1)
            for h in range(2):
                dve.wait_ge(S["turn_ready"], h + 1)
                V.tensor_scalar(WT[:, h * 512:(h + 1) * 512], bank[4 + h][0:D, :], sigma[:], None, ALU.mult)\
                    .then_inc(S["turned_ready"], 1)

            def norm_stats(src, b):
                seq(V.bn_stats(stats[:, b, :], src))
                V.bn_aggr(mv[:, b, :], stats[:, b, :]).then_inc(S["var_ready"], 1)

            def normalized(src, ln):
                dve.wait_ge(S["var_ready"], B * (ln + 1))
                dve.wait_ge(S["rstd_ready"], ln + 1)
                if ln:
                    dve.wait_ge(S["hT_mm"], B)
                for b in range(B):
                    V.tensor_scalar(H[:, b, :], src[:, b, :], mv[:, b, 0:1], rstd[:, b:b + 1],
                                    ALU.subtract, ALU.mult).then_inc(S["h_ready"], 1)

            for b in range(B):
                dve.wait_ge(S["delta_ready"], b + 1)
                V.tensor_tensor(XR[:, b, :], bank[b % 2][:, 0:C], x_in[:, b, :], ALU.add).then_inc(S["xr_used"], 1)
                dve.wait_ge(S["xr_used"], b + 1)
                norm_stats(XR[:, b, :], b)
            normalized(XR, 0)
            dve.wait_ge(S["ones_set"], 3)
            for b in range(B):
                dve.wait_ge(S["proj_mm"], 16 + b + 1)
                V.tensor_copy(VA[:, b, :, 0:HD], bank[2 + b % 2][:, 0:C].rearrange("p (h d) -> p h d", h=NH))\
                    .then_inc(S["v_sb"], 1)
            dve.wait_ge(S["nm_zero"], 1)

            def maxima(b):
                for t in range(HEAD_SLOTS):
                    dve.wait_ge(S["scoreA"], 4 * b + t + 1)
                    if b >= 2 and t == 0:
                        dve.wait_ge(S["mxT_mm"], b - 1)
                    dst = NM[:, b % 2, :, t * STRIP + HD]
                    V.tensor_reduce(dst, bank[t % 2][:, :].rearrange("p (t k) -> p t k", t=HEAD_SLOTS), AX_X, ALU.max,
                                    negate=True).then_inc(S["mx_ready"], 1)

            def shifts(b):
                dve.wait_ge(S["mxT_mm"], b + 1)
                q = QT[:, :, b * T:(b + 1) * T]
                V.tensor_tensor(q, bank[4][:, :].rearrange("p (t q) -> p t q", t=HEAD_SLOTS), q, ALU.add)\
                    .then_inc(S["qm_ready"], 1)

            maxima(0)
            for b in range(B):
                if b + 1 < B:
                    maxima(b + 1)
                shifts(b)
                dve.wait_ge(S["pv_mm"], b + 1)
                o = bank[5][:, 0:NH * VW].rearrange("p (h d) -> p h d", h=NH)
                seq(V.reciprocal(rsum[:, b % 2, :], o[:, :, HD]))
                if b >= 2:
                    dve.wait_ge(S["oT_mm"], b - 1)
                V.tensor_tensor(OA[:, b % 2, :].rearrange("p (h d) -> p h d", h=NH), o[:, :, 0:HD],
                                rsum[:, b % 2, :].unsqueeze(2).to_broadcast([P, NH, HD]), ALU.mult)\
                    .then_inc(S["o_ready"], 1)
                dve.wait_ge(S["gate_sb"], B)
                dve.wait_ge(S["attn_mm"], b + 1)
                seq(V.tensor_tensor(PG[:, b % 2, :], bank[7][:, 0:C], GB[:, b, 0, :], ALU.mult))
                V.tensor_tensor(X2[:, b, :], PG[:, b % 2, :], XR[:, b, :], ALU.add).then_inc(S["x2_ready"], 1)
                dve.wait_ge(S["x2_ready"], b + 1)
                norm_stats(X2[:, b, :], b)
            normalized(X2, 1)

            dve.wait_ge(S["lg_sb"], 1)
            other = lg[:].unsqueeze(2).to_broadcast([P, B, NE, NE])
            own = lg[:].unsqueeze(3).to_broadcast([P, B, NE, NE])
            seq(V.tensor_tensor(gt[:], other, own, ALU.is_gt))
            seq(V.tensor_tensor(eq[:], other, own, ALU.is_equal))
            ties = rank_ties.unsqueeze(1).to_broadcast([P, B, NE * NE])
            eqf = eq[:].rearrange("p b e f -> p b (e f)")
            seq(V.tensor_tensor(eqf, eqf, ties, ALU.mult))
            seq(V.tensor_tensor(gt[:], gt[:], eq[:], ALU.add))
            seq(V.tensor_reduce(rank[:], gt[:], AX_X, ALU.add))
            seq(V.tensor_scalar(rank[:], rank[:], 1.5, None, ALU.is_lt))
            seq(V.tensor_reduce(gmax[:], lg[:], AX_X, ALU.max))
            V.tensor_tensor(sel[:], lg[:], gmax[:].unsqueeze(2).to_broadcast([P, B, NE]), ALU.subtract)\
                .then_inc(S["x2_ready"], 1)
            dve.wait_ge(S["lg_sb"], 2)
            seq(V.tensor_tensor(sel[:], sel[:], rank[:], ALU.mult))
            seq(V.tensor_reduce(gsum[:], sel[:], AX_X, ALU.add))
            seq(V.reciprocal(rgs[:], gsum[:]))
            V.tensor_tensor(cw[:], sel[:], rgs[:].unsqueeze(2).to_broadcast([P, B, NE]), ALU.mult)\
                .then_inc(S["cw_ready"], 1)
            dve.wait_ge(S["cw_ready"], 1)
            for b in range(B):
                acc = ACC[:, b % 2, :]
                dve.wait_ge(S["down_mm"], 2 * b + 2)
                seq(V.tensor_copy(acc, bank[5][:, 0:C]))
                for e in range(NE):
                    src = bank[3 + e // 2][:, (e % 2) * C:(e % 2 + 1) * C]
                    ins = V.scalar_tensor_tensor(acc, src, cw[:, b, e:e + 1], acc, ALU.mult, ALU.add)
                    if e == NE - 1:
                        ins.then_inc(S["down_used"], 1)
                        dve.wait_ge(S["down_used"], b + 1)
                    else:
                        seq(ins)
                seq(V.tensor_tensor(acc, acc, GB[:, b, 1, :], ALU.mult))
                V.tensor_tensor(RES[:, b, :], acc, X2[:, b, :], ALU.add).then_inc(S["res_ready"], 1)


def _layout(inputs):
    import numpy as np
    f = {k: np.asarray(v) for k, v in inputs.items()}
    ones = lambda n: np.ones((1, n), np.float32)

    def with_bias(w, b):
        return np.ascontiguousarray(np.concatenate([w, b.reshape(1, -1)], 0))

    x = np.ascontiguousarray(f["x"])
    iu, ju = np.triu_indices(D, k=1)
    rot = np.zeros((C + 1, D, D), np.float32)
    rows = with_bias(f["L0_cond_W"].T, f["L0_cond_b"])
    rot[:, ju, iu] = rows
    rot[:, iu, ju] = rows
    qkv = with_bias(f["L1_cond_w_qkv"], f["L1_cond_b_qkv"])

    def strips(part, extra):
        w = np.zeros((C + 1, HEAD_SLOTS, STRIPS, STRIP), np.float32)
        w[:, :, :, 0:HD] = qkv[:, part * C:(part + 1) * C]\
            .reshape(C + 1, STRIPS, HEAD_SLOTS, HD).transpose(0, 2, 1, 3)
        w[C, :, :, HD] = extra
        return w.reshape(C + 1, HEAD_SLOTS * P)

    w1 = f["L1_cond_w1"].transpose(1, 0, 2).reshape(C, NE * HID)
    c = np.zeros((P, 384), np.float32)
    c[:, 0:P] = np.eye(P)
    i = np.arange(D)
    c[0:D, 128:192] = 0.5 * np.eye(D)
    c[0:D, 192:256] = -(i[:, None] > i[None, :]).astype(np.float32)
    c[0:D, 256:320] = np.sign(i[None, :] - i[:, None])
    c[:, 320:320 + NSQ] = 2.0 ** (np.arange(NSQ) + 1)
    c[:, 340:340 + NSQ] = 2.0 ** -(np.arange(NSQ) + 1.0)
    e = np.arange(NE)
    c[:, 360:376] = (e[None, :] < e[:, None]).astype(np.float32).reshape(1, NE * NE)
    return {
        "xtok": x, "xT": np.ascontiguousarray(x.reshape(B * T, C).T),
        "pmat": f["L0_cond_P"], "pT": np.ascontiguousarray(f["L0_cond_P"].T),
        "condT": np.concatenate([f["cond_1152"].T, ones(B)], 0),
        "rotW": rot.reshape(C + 1, D * D),
        "adaW": with_bias(f["L1_cond_w_adaln"], f["L1_cond_b_adaln"]),
        "wq": strips(0, 0.0), "wk": strips(1, 1.0),
        "wv": np.ascontiguousarray(qkv[:, 2 * C:]),
        "wproj": with_bias(f["L1_cond_w_proj"], f["L1_cond_b_proj"]),
        "wgate": f["L1_cond_w_gate"],
        "w1": with_bias(w1, f["L1_cond_b1"]),
        "w2": f["L1_cond_w2"], "b2": f["L1_cond_b2"], "consts": c,
    }


def kernel(**inputs):
    import numpy as _np
    import concourse.bacc as _bacc
    from concourse import mybir as _mybir
    from concourse.bass_utils import run_bass_kernel_spmd as _run

    nc = _bacc.Bacc("TRN2", target_bir_lowering=False, num_devices=1)
    arrays, args = {}, {}
    for name, a in _layout(inputs).items():
        a = _np.ascontiguousarray(a)
        arrays[f"in_{name}"] = a
        args[name] = nc.dram_tensor(f"in_{name}", a.shape, _mybir.dt.from_np(a.dtype), kind="ExternalInput").ap()
    out = nc.dram_tensor("out", (B, T, C), _mybir.dt.from_np(_np.dtype("float32")), kind="ExternalOutput").ap()
    bass_conditional_rotation_moe_block(nc, out=out, **args)
    r = _run(nc, [arrays], core_ids=[0])
    return r.results[0]["out"]
```

```python
from contextlib import ExitStack

import concourse.bass as bass
from concourse import mybir

ALU = mybir.AluOpType
ACT = mybir.ActivationFunctionType
F32 = mybir.dt.float32
I32 = mybir.dt.int32
BF16 = mybir.dt.bfloat16
AX_X = mybir.AxisListType.X
RMAX = bass.bass_isa.ReduceOp.max

P = 128
B, T, C = 8, 128, 144
D = 64
NH, HD = 16, 9
NE, HID = 4, 576
R = C - P
RA = R + 1
NSQ = 18
NTERM = 8
SLOTS = 6
WPART = (3, 2, 1, 1, 1, 2)
RS = SLOTS * R
RK = RS + 3
HK = 64
DK = SLOTS * HD
DM = DK + 2
VW = 32
LN_EPS = 1e-6
QK_SCALE = float(HD) ** -0.5
UP = NE * HID // P
UP_BEFORE_NORM, UP_BEFORE_LOGITS, UP_BEFORE_EXP = 5, 9, 12
HALF = 4 * T
N_ST = 3 * C + NE + NE * HID
ST_COLS = N_ST // 10


def steps(now, then):
    return (None for _ in range(then - now))


def factorial(n):
    out = 1.0
    for i in range(2, n + 1):
        out *= i
    return out


def bass_conditional_rotation_moe_block(nc, xtok, xT, pmat, pT, condT, rotW, adaW, wmain, wproj, wstack,
                                        w2, b2, consts, rotR, condR, out):
    with ExitStack() as ctx:
        def sb(name, shape, dt=F32):
            return ctx.enter_context(nc.sbuf_tensor(name, shape, dt))

        def sem(name):
            return ctx.enter_context(nc.semaphore(name))

        bank = [ctx.enter_context(nc.psum_tensor(f"bank{i}", [P, 512], F32)) for i in range(8)]

        cst = sb("cst", [P, consts.shape[1]])
        ident = cst[:, 0:P]
        id64 = cst[0:D, 0:D]
        id_stacked = cst[:, 392:392 + D]
        rot_bias = cst[:, 456:456 + D]
        half_id = cst[0:D, 128:192]
        below = cst[0:D, 192:256]
        skew_sign = cst[:, 256:320]
        thresholds = cst[:, 320:320 + NSQ]
        halvings = cst[:, 340:340 + NSQ]
        rank_ties = cst[:, 360:376]
        minus_23, minus_3 = cst[0:RK, 380:381], cst[0:RK, 381:382]
        identb = sb("identb", [P, P], BF16)
        P_m, P_r = sb("P_m", [P, D]), sb("P_r", [R, D])
        PT = sb("PT", [D, C])
        early = sb("early", [P, 2 * B * T])
        xT_m, xT_r = early[:, 0:B * T], early[0:R, B * T:2 * B * T]
        x_in = sb("x_in", [P, B, C])
        s_m, s_r = sb("s_m", [P, B]), sb("s_r", [RA, B])
        s_diag = sb("s_diag", [P, 8 * B])
        shared = sb("shared", [P, 12288])
        rot_m = shared[:, 0:D * D].rearrange("p (j o) -> p j o", j=D // 2)
        rot_r = shared[:, D * D:D * D + 4 * P].rearrange("p (g o) -> p g o", g=4)
        QKS = shared[:, 0:8192].bitcast(BF16).rearrange("p (b g h c) -> p b g h c", b=B, g=2, h=NH)
        PR = shared[:, 8192:12288].rearrange("p (s h q) -> p s h q", s=2, h=NH)
        HM = shared[:, 0:UP * HALF].rearrange("p (j n) -> p j n", j=UP)
        ada_m, ada_r = sb("ada_m", [P, 6 * C]), sb("ada_r", [RA, 6 * C])
        wm = sb("wm", [P, 3 * C + NE + NE * HID])
        wqkv_m, wg_m, w1_m = wm[:, 0:3 * C], wm[:, 3 * C:3 * C + NE], wm[:, 3 * C + NE:]
        wst32, wst = sb("wst32", [RK, N_ST]), sb("wst", [RK, N_ST], BF16)
        wqkv_s, wg_s, w1_s = wst[:, 0:3 * C], wst[:, 3 * C:3 * C + NE], wst[:, 3 * C + NE:]
        wp_m, wp_r = sb("wp_m", [P, C]), sb("wp_r", [RA, C])
        w2_s = sb("w2_s", [P, UP, C])
        b2_s = sb("b2_s", [NE, C])

        EL = sb("EL", [D, 2 * D])
        rpiv, coef = sb("rpiv", [D, 2]), sb("coef", [D, 2])
        rnrm, rnrm_below = sb("rnrm", [D, 2]), sb("rnrm_below", [D, 2])
        piv, rnorm = sb("piv", [D, 1]), sb("rnorm", [D, 1])
        mhalf = sb("mhalf", [P, B])
        LT = sb("LT", [D, D])
        xPT = sb("xPT", [D, B * T])
        U0T = sb("U0T", [D, C])
        Z0T = sb("Z0T", [P, HALF])
        TOP = sb("TOP", [D, D])
        SG = sb("SG", [D, D])
        sized, lead, rlead = sb("sized", [D, 1]), sb("lead", [D, 1]), sb("rlead", [D, 1])
        scaled, reflected, tcoef = sb("scaled", [D, 1]), sb("reflected", [D, 1]), sb("tcoef", [D, 1])
        diagonal, sign_of = sb("diagonal", [D, D]), sb("sign_of", [D, D])
        sigma, signed_rnorm = sb("sigma", [D, 1]), sb("signed_rnorm", [D, 1])
        LN = sb("LN", [D, D])

        A = sb("A", [P, 4, D])
        quadrant = sb("quadrant", [P, 4, D // 2])
        norms, norm8, norm = sb("norms", [P, B]), sb("norm8", [P, B]), sb("norm", [P, 4])
        active = sb("active", [P, NSQ, 4])
        shrink, scale = sb("shrink", [P, 4, NSQ]), sb("scale", [P, 4])
        series = sb("series", [P, B * NH * VW])
        A_diag, N1_diag, N2_diag, N4_diag = (series[:, i * 4 * P:(i + 1) * 4 * P].rearrange("p (b j) -> p b j", b=4)
                                             for i in range(4))
        N1, N2, Chi, Dhi, Clo, Dlo = (series[:, 16 * P + i * 4 * D:16 * P + (i + 1) * 4 * D]
                                      .rearrange("p (b j) -> p b j", b=4) for i in range(6))
        X, X_diag = sb("X", [P, 2, 4, D]), sb("X_diag", [P, 2, 4, P])
        WT = sb("WT", [D, B * T])

        MOD = sb("MOD", [P, 4, B])
        gate_rows = nc.dram_tensor("gate_rows", (B, 2 * C + 6 * R), F32).ap()
        gates8 = sb("gates8", [B, 2 * C + 6 * R])
        GM = sb("GM", [P, B, 2 * C + 6 * R])
        GB = GM[:, :, 0:2 * C].rearrange("p b (g c) -> p b g c", g=2)
        MB = GM[:, :, 2 * C:].rearrange("p b (g c) -> p b g c", g=6)
        XR = sb("XR", [P, B, C])
        stats = sb("stats", [P, B, 6])
        mv = sb("mv", [P, 2, B, 2])
        veps, rstd = sb("veps", [P, 2, B]), sb("rstd", [P, 2, B])
        H = sb("H", [P, B, C])
        hr, hres = sb("hr", [P, 4, R]), sb("hres", [P, 4, R])
        HS = sb("HS", [P, B, RK], BF16)
        HT = sb("HT", [P, B * T])
        HST = sb("HST", [RK, B * T], BF16)
        qkres = sb("qkres", [P, B, 2 * C])
        qkres2 = sb("qkres2", [P, 2, 2 * C])
        QT = sb("QT", [P, 2, NH // 2, T], BF16)
        KT = early[:, :].bitcast(BF16).rearrange("p (s h i k) -> p s h i k", s=2, h=NH // 2, i=2)
        VA = series[:, :].rearrange("p (b h d) -> p b h d", b=B, h=NH)
        nmax, nmres = sb("nmax", [P, NH]), sb("nmres", [P, NH])
        OS = sb("OS", [P, 4, T])
        rsum = sb("rsum", [P, 2, NH])
        OA = sb("OA", [P, 2, C])
        OT_m, OT_r = sb("OT_m", [P, 2, T]), sb("OT_r", [RA, 2, T])
        PG = sb("PG", [P, 2, C])
        X2 = sb("X2", [P, B, C])
        lg = sb("lg", [P, B, NE])
        gt, eq = sb("gt", [P, B, NE, NE]), sb("eq", [P, B, NE, NE])
        rank = sb("rank", [P, B, NE])
        gmax = sb("gmax", [P, B])
        gsum, rgs = sb("gsum", [P, B]), sb("rgs", [P, B])
        sel = sb("sel", [P, B, NE])
        cw = sb("cw", [P, B, NE])
        cwT = xPT[0:NE, :]
        ACC = sb("ACC", [P, 2, C])

        in_cst, in_qr, in_cond, in_rot, in_x, in_ada, in_attn, in_moe, gates_in = (sem(n) for n in (
            "in_cst", "in_qr", "in_cond", "in_rot", "in_x", "in_ada", "in_attn", "in_moe", "gates_in"))
        dve_done = sem("dve_done")
        pool_done = sem("pool_done")
        silu_done = sem("silu_done")
        names = ("gram_ready ln_ready z_sb row_ready row_used rpiv_ready coef_ready rnrm_step rnrm_ready linv_ready linvT_ready lT_ready basis_ready top_ready top_used "
                 "a_ready a_diag ent_ready staged quad_sb quad_in norms_ready norm_ready n1_mm n1_sb n2_mm n2_sb n3_mm n3_sb "
                 "n4_sb hi_ready hi_mm cd_ready ad_mm x_ready x_step x_diag sq_mm diag_zeroed gates_ready "
                 "piv_ready rnorm_ready xp_ready xp_sb z_ready turn_ready turned_ready turned_hi delta_ready zeroed "
                 "f_ready xr_used var_ready rstd_ready h_ready hs_ready hT_mm hT_sb mod_mm mod_sb gate_mm gate_sb "
                 "identb_ready wst_step wst_ready qkv_mm qk1_sb r1_ready qk_used pool_step stack_ready v_sb ms_zero "
                 "qkT_mm qkT_sb scoreA mx_ready ms_ready mxT_mm mxT_sb scoreB pr_ready pv_mm os_sb back_mm o_ready "
                 "oT_mm oT_sb attn_mm x2_ready lg_mm lg_sb sel_ready exp_ready cw_ready cwT_mm cwT_sb up_mm "
                 "act_ready down_mm down_used res_ready stored").split()
        S = {n: sem(n) for n in names}

        cosc = [(-1.0) ** i / factorial(2 * i) for i in range(NTERM)]
        sinc = [(-1.0) ** i / factorial(2 * i + 1) for i in range(NTERM)]

        block = ctx.enter_context(nc.Block())

        def rt(ap, b):
            return ap[:, b * T:(b + 1) * T]

        @block.sync
        def _(sp):
            sp.dma_start(cst[:], consts).then_inc(in_cst, 16)
            sp.dma_start(P_m[:], pmat[0:P, :]).then_inc(in_qr, 16)
            sp.dma_start(P_r[:], pmat[P:C, :]).then_inc(in_qr, 16)
            sp.dma_start(PT[:], pT).then_inc(in_qr, 16)
            sp.dma_start(s_m[:], condT[0:P, :]).then_inc(in_cond, 16)
            sp.dma_start(s_r[:], condT[P:C + 1, :]).then_inc(in_cond, 16)
            sp.dma_start(s_diag[:], condR).then_inc(in_cond, 16)
            sp.dma_start(ada_m[:], adaW[0:P, :]).then_inc(in_ada, 16)
            sp.dma_start(ada_r[:], adaW[P:C + 1, :]).then_inc(in_ada, 16)
            sp.dma_start(shared[:, 0:D * D], rotW).then_inc(in_rot, 16)
            sp.dma_start(shared[:, D * D:D * D + 4 * P], rotR).then_inc(in_rot, 16)
            sp.dma_start(xT_m, xT[0:P, :]).then_inc(in_x, 16)
            sp.dma_start(xT_r, xT[P:C, :]).then_inc(in_x, 16)
            sp.dma_start(x_in[:], xtok.rearrange("b t c -> t b c")).then_inc(in_x, 16)
            sp.dma_start(wst32[:], wstack).then_inc(in_attn, 16)
            sp.dma_start(wp_m[:], wproj[0:P, :]).then_inc(in_moe, 16)
            sp.dma_start(wp_r[:], wproj[P:C + 1, :]).then_inc(in_moe, 16)
            sp.dma_start(wm[:], wmain).then_inc(in_moe, 16)
            sp.dma_start(w2_s[:], w2.rearrange("(t p) c -> p t c", p=P))\
                .then_inc(in_moe, 16)
            sp.dma_start(b2_s[:], b2).then_inc(in_moe, 16)
            sp.wait_ge(S["staged"], 2)
            sp.dma_start(A[D:P, :, 0:D // 2], quadrant[0:D, :, :]).then_inc(S["quad_in"], 16)
            sp.dma_start(A[0:D, :, D // 2:D], quadrant[D:P, :, :]).then_inc(S["quad_in"], 16)
            sp.wait_ge(S["gates_ready"], 2)
            sp.dma_start(gate_rows, gates8[:]).then_inc(gates_in, 16)
            sp.wait_ge(gates_in, 16)
            sp.dma_start(GM[:], gate_rows.unsqueeze(0).to_broadcast([P, B, 2 * C + 6 * R])).then_inc(gates_in, 16)
            for b in range(B):
                sp.wait_ge(S["res_ready"], b + 1)
                sp.dma_start(out[b], X2[:, b, :]).then_inc(S["stored"], 16)
            sp.wait_ge(S["stored"], 16 * B)
        N_MOE = 16 * 5

        @block.gpsimd
        def _(pool):
            nc.gpsimd.memset(mhalf[:], -0.5).then_inc(pool_done, 1)
            nc.gpsimd.memset(norms[:], 0.0).then_inc(S["diag_zeroed"], 1)
            nc.gpsimd.memset(X_diag[:].rearrange("p e b j -> p (e b j)"), 0.0).then_inc(S["diag_zeroed"], 1)
            nc.gpsimd.memset(series[:, 0:16 * P], 0.0).then_inc(S["diag_zeroed"], 1)

            def beside_elimination():
                yield
                nc.gpsimd.memset(HS[:], 1.0).then_inc(S["zeroed"], 1)
                yield
                nc.gpsimd.memset(OT_r[:], 1.0).then_inc(S["zeroed"], 1)
                yield from steps(2, 16)
                pool.wait_ge(S["norms_ready"], 2)
                nc.gpsimd.partition_all_reduce(norm8[:], norms[:], P, RMAX).then_inc(S["norm_ready"], 1)
                yield
                for h in range(2):
                    pool.wait_ge(S["xp_ready"], 2)
                    nc.gpsimd.memset(early[:, h * B * T:(h + 1) * B * T], 0.0).then_inc(S["zeroed"], 1)
                    yield
                pool.wait_ge(in_cst, 16)
                pool.wait_ge(in_attn, 16)
                n = 0
                for c in range(0, N_ST, ST_COLS):
                    part, whole = wst[:, c:c + ST_COLS], wst32[:, c:c + ST_COLS]
                    for minus in (minus_23, minus_3):
                        yield
                        nc.gpsimd.tensor_copy(part, whole).then_inc(S["wst_step"], 1)
                        yield
                        pool.wait_ge(S["wst_step"], n + 1)
                        nc.gpsimd.tensor_scalar(part, part, minus, None, ALU.mult).then_inc(S["wst_step"], 1)
                        yield
                        pool.wait_ge(S["wst_step"], n + 2)
                        nc.gpsimd.tensor_tensor(whole, whole, part, ALU.add).then_inc(S["wst_step"], 1)
                        n += 3
                        pool.wait_ge(S["wst_step"], n)
                    yield
                    nc.gpsimd.tensor_copy(part, whole).then_inc(S["wst_ready"], 1)

            beside = beside_elimination()
            for k in range(D - 1):
                pool.wait_ge(S["rpiv_ready"], k + 1)
                pool.wait_ge(S["row_used"], k + 1)
                nc.gpsimd.tensor_scalar(coef[:, k % 2:k % 2 + 1], EL[:, k:k + 1], rpiv[:, k % 2:k % 2 + 1],
                                        below[:, k:k + 1], ALU.mult, ALU.mult).then_inc(S["coef_ready"], 1)
                next(beside, None)
            pool.wait_ge(S["piv_ready"], 1)
            pool.wait_ge(pool_done, 1)
            nc.gpsimd.tensor_tensor(rnorm[:], piv[:], mhalf[0:D, 0:1], ALU.pow).then_inc(S["rnorm_ready"], 1)
            pool.wait_ge(S["ent_ready"], 1)
            nc.gpsimd.memset(QKS[:, :, :, :, DK:HK].rearrange("p b g h c -> p (b g h) c"), 0.0)\
                .then_inc(pool_done, 1)
            pool.wait_ge(pool_done, 2)
            nc.gpsimd.memset(QKS[:, :, 1, :, DK:DM], 1.0).then_inc(S["zeroed"], 1)
            pool.wait_ge(S["x_ready"], 2)
            nc.gpsimd.memset(series[:, :], 0.0).then_inc(pool_done, 1)
            pool.wait_ge(pool_done, 3)
            nc.gpsimd.memset(VA[:, :, :, HD:HD + 1], 1.0).then_inc(S["zeroed"], 1)

            def inverse_deviations(ln, h):
                u = 2 * ln + h
                pool.wait_ge(S["var_ready"], 4 * (u + 1))
                nc.gpsimd.tensor_scalar(veps[:, ln, 4 * h:4 * h + 4], mv[:, ln, 4 * h:4 * h + 4, 1], LN_EPS, None,
                                        ALU.add).then_inc(pool_done, 1)
                pool.wait_ge(pool_done, 4 + u)
                nc.gpsimd.tensor_tensor(rstd[:, ln, 4 * h:4 * h + 4], veps[:, ln, 4 * h:4 * h + 4], mhalf[:, 0:4],
                                        ALU.pow).then_inc(S["rstd_ready"], 1)

            inverse_deviations(0, 0)
            inverse_deviations(0, 1)
            for b in range(B):
                pool.wait_ge(S["r1_ready"], b + 1)
                st = QKS[:, b].rearrange("p g h c -> p g h c")
                res = qkres[:, b, :].rearrange("p (g h d) -> p g h d", g=2, h=NH)

                def slots(g, first, stride, n):
                    return st[:, g, :, 0:DK].rearrange("p h (s d) -> p h s d", s=SLOTS)[:, :, first:first + stride * (n - 1) + 1:stride, :]

                def wide(x, g, n):
                    return x[:, g].unsqueeze(2).to_broadcast([P, NH, n, HD])
                nc.gpsimd.tensor_copy(slots(0, 3, 2, 2), wide(res, 0, 2)).then_inc(S["pool_step"], 1)
                nc.gpsimd.tensor_copy(slots(1, 1, 4, 2), wide(res, 1, 2)).then_inc(S["pool_step"], 1)
                pool.wait_ge(S["pool_step"], 3 * b + 2)
                part2 = QKS[:, b, :, :, 5 * HD:6 * HD].rearrange("p g h d -> p (g h) d")
                r32 = qkres[:, b, :].rearrange("p (g d) -> p g d", d=HD)
                res2 = qkres2[:, b % 2, :].rearrange("p (g d) -> p g d", d=HD)
                nc.gpsimd.tensor_tensor(res2, r32, part2, ALU.subtract).then_inc(S["pool_step"], 1)
                pool.wait_ge(S["pool_step"], 3 * b + 3)
                res2 = qkres2[:, b % 2, :].rearrange("p (g h d) -> p g h d", g=2, h=NH)
                nc.gpsimd.tensor_copy(QKS[:, b, 0, :, 4 * HD:5 * HD], res2[:, 0]).then_inc(S["stack_ready"], 1)
                nc.gpsimd.tensor_copy(QKS[:, b, 1, :, 0:HD], res2[:, 1]).then_inc(S["stack_ready"], 1)
            for _ in beside:
                pass
            inverse_deviations(1, 0)
            inverse_deviations(1, 1)

        @block.scalar
        def _(act):
            act.wait_ge(in_cond, 48)
            nc.scalar.activation(s_m[:], s_m[:], ACT.Silu).then_inc(silu_done, 1)
            nc.scalar.activation(s_r[0:R, :], s_r[0:R, :], ACT.Silu).then_inc(silu_done, 1)
            nc.scalar.activation(s_diag[:], s_diag[:], ACT.Silu).then_inc(silu_done, 1)

            def diagonal_blocks(dst, src):
                nc.scalar.activation(dst[0:D, ..., 0:D], src[0:D], ACT.Copy)
                return nc.scalar.activation(dst[D:P, ..., D:P], src[D:P], ACT.Copy)

            def pairs(src):
                return src.rearrange("p (b j) -> p b j", b=4)

            def beside_elimination():
                yield from steps(0, 5)
                act.wait_ge(S["gate_mm"], 1)
                nc.scalar.activation(gates8[:], bank[4][0:B, 0:2 * C + 6 * R], ACT.Copy).then_inc(S["gate_sb"], 1)
                yield from steps(5, 12)
                act.wait_ge(S["ent_ready"], 1)
                ent = bank[2][:, 0:D // 2 * B].rearrange("p (j h b) -> p h b j", h=2, b=4)
                nc.scalar.activation(quadrant[0:D], ent[0:D, 1], ACT.Copy).then_inc(S["staged"], 1)
                nc.scalar.activation(quadrant[D:P], ent[D:P, 0], ACT.Copy).then_inc(S["staged"], 1)
                nc.scalar.activation(A[0:D, :, 0:D // 2], ent[0:D, 0], ACT.Copy)
                nc.scalar.activation(A[D:P, :, D // 2:D], ent[D:P, 1], ACT.Copy).then_inc(S["quad_sb"], 1)
                for h in range(2):
                    yield from steps(12, 14)
                    act.wait_ge(S["xp_ready"], h + 1)
                    nc.scalar.activation(xPT[:, h * 512:(h + 1) * 512], bank[6 + h][0:D, :], ACT.Copy)\
                        .then_inc(S["xp_sb"], 1)
                yield from steps(16, 19)
                act.wait_ge(S["diag_zeroed"], 3)
                act.wait_ge(S["a_ready"], 1)
                diagonal_blocks(A_diag, A).then_inc(S["a_diag"], 1)
                yield from steps(19, 21)
                act.wait_ge(S["n1_mm"], 1)
                diagonal_blocks(N1_diag, pairs(bank[3][:, 0:4 * D]))
                nc.scalar.activation(N1, pairs(bank[3][:, 0:4 * D]), ACT.Copy).then_inc(S["n1_sb"], 1)
                yield
                act.wait_ge(S["n2_mm"], 1)
                diagonal_blocks(N2_diag, pairs(bank[4][:, 0:4 * D]))
                nc.scalar.activation(N2, pairs(bank[4][:, 0:4 * D]), ACT.Copy).then_inc(S["n2_sb"], 1)
                yield
                act.wait_ge(S["n3_mm"], 1)
                for p, c in ((Chi, cosc[7]), (Dhi, sinc[7]), (Clo, cosc[3]), (Dlo, sinc[3])):
                    nc.scalar.activation(p, pairs(bank[3][:, 0:4 * D]), ACT.Copy, scale=c).then_inc(S["n3_sb"], 1)
                yield
                act.wait_ge(S["n3_mm"], 2)
                diagonal_blocks(N4_diag, pairs(bank[4][:, 0:4 * D])).then_inc(S["n4_sb"], 1)
                yield from steps(24, 30)
                act.wait_ge(S["x_ready"], 2)
                for h in range(2):
                    diagonal_blocks(X_diag[:, :, 2 * h:2 * h + 2, :], X[:, :, 2 * h:2 * h + 2, :])\
                        .then_inc(S["x_diag"], 1)
                yield
                for n in range(2 * (NSQ - 1)):
                    yield
                    h = n % 2
                    act.wait_ge(S["x_step"], n + 1)
                    diagonal_blocks(X_diag[:, :, 2 * h:2 * h + 2, :], X[:, :, 2 * h:2 * h + 2, :])\
                        .then_inc(S["x_diag"], 1)

            beside = beside_elimination()
            for k in range(D - 1):
                act.wait_ge(S["rpiv_ready"], k + 1)
                col = slice(k % 2, k % 2 + 1)
                nc.scalar.activation(rnrm[:, col], rpiv[:, col], ACT.Sqrt).then_inc(S["rnrm_step"], 1)
                act.wait_ge(S["rnrm_step"], k + 1)
                nc.scalar.activation(rnrm_below[:, col], below[:, k:k + 1], ACT.Copy, scale=rnrm[:, col])\
                    .then_inc(S["rnrm_ready"], 1)
                next(beside, None)
            for _ in beside:
                pass
            act.wait_ge(S["turn_ready"], 2)
            nc.scalar.activation(WT[:, HALF:2 * HALF], bank[5][0:D, :], ACT.Copy).then_inc(S["turned_hi"], 1)

            def modulated(ln, h):
                u = 2 * ln + h
                act.wait_ge(S["hT_mm"], u + 1)
                lo = ((2, 0), (0, 3))[ln][h]
                for b in range(4):
                    nc.scalar.activation(rt(HT, 4 * h + b), bank[lo][:, b * T:(b + 1) * T], ACT.Identity,
                                         bias=MOD[:, 2 * ln, 4 * h + b:4 * h + b + 1],
                                         scale=MOD[:, 2 * ln + 1, 4 * h + b:4 * h + b + 1])
                nc.scalar.activation(HST[:, h * HALF:(h + 1) * HALF], bank[lo + 1][0:RK, 0:HALF // 2].bitcast(BF16),
                                     ACT.Copy).then_inc(S["hT_sb"], 1)

            act.wait_ge(S["mod_sb"], 1)
            modulated(0, 0)
            act.wait_ge(S["zeroed"], 6)
            for b in range(B):
                if b == 4:
                    modulated(0, 1)
                act.wait_ge(S["qkv_mm"], b + 1)
                qkv = bank[4 + b % 4][:, 0:2 * C].rearrange("p (g h d) -> p g h d", g=2, h=NH)
                for g, first in ((0, 0), (1, 2)):
                    dst = QKS[:, b, g, :, first * HD:(first + 3) * HD].rearrange("p h (s d) -> p h s d", s=3)
                    last = nc.scalar.activation(dst, qkv[:, g].unsqueeze(2).to_broadcast([P, NH, 3, HD]), ACT.Copy)
                last.then_inc(S["qk1_sb"], 1)

            def out_transposed(b):
                act.wait_ge(S["oT_mm"], b + 1)
                if b >= 2:
                    act.wait_ge(S["attn_mm"], b - 1)
                nc.scalar.activation(OT_m[:, b % 2, :], bank[6][:, 0:T], ACT.Copy)
                nc.scalar.activation(OT_r[0:R, b % 2, :], bank[6][0:R, T:2 * T], ACT.Copy).then_inc(S["oT_sb"], 1)

            def shifted(b):
                act.wait_ge(S["mxT_mm"], b + 1)
                nc.scalar.activation(QT[:, b % 2, :, :].rearrange("p h q -> p (h q)"),
                                     bank[7][:, :].bitcast(BF16), ACT.Copy).then_inc(S["mxT_sb"], 1)

            shifted(0)
            for b in range(B):
                for g in range(4):
                    act.wait_ge(S["scoreB"], b * 4 + g + 1)
                    if b >= 2 and g == 0:
                        act.wait_ge(S["pv_mm"], b - 1)
                    nc.scalar.activation(PR[:, b % 2, 4 * g:4 * g + 4, :],
                                         bank[4 + g % 2][:, :].rearrange("p (h q) -> p h q", h=4),
                                         ACT.Exp, scale=QK_SCALE).then_inc(S["pr_ready"], 1)
                    if g == 0 and b >= 1:
                        out_transposed(b - 1)
                if b + 1 < B:
                    shifted(b + 1)
                act.wait_ge(S["pv_mm"], b + 1)
                if b >= 1:
                    act.wait_ge(S["back_mm"], b)
                nc.scalar.activation(OS[:].rearrange("p j q -> p (j q)"), bank[6][:, :], ACT.Copy)\
                    .then_inc(S["os_sb"], 1)
                if b == B - 1:
                    modulated(1, 0)
            out_transposed(B - 1)

            def gelu(h, j):
                n = h * UP + j
                act.wait_ge(S["up_mm"], n + 1)
                if h and j == 0:
                    act.wait_ge(S["down_mm"], 4)
                nc.scalar.activation(HM[:, j, :], bank[n % 3][:, :], ACT.Gelu_apprx_tanh)\
                    .then_inc(S["act_ready"], 1)

            for j in range(UP_BEFORE_NORM):
                gelu(0, j)
            modulated(1, 1)
            for j in range(UP_BEFORE_NORM, UP_BEFORE_LOGITS):
                gelu(0, j)
            act.wait_ge(S["lg_mm"], 1)
            nc.scalar.activation(lg[:], bank[7][:, 0:B * NE].rearrange("p (b e) -> p b e", b=B), ACT.Copy)\
                .then_inc(S["lg_sb"], 1)
            for j in range(UP_BEFORE_LOGITS, UP_BEFORE_EXP):
                gelu(0, j)
            act.wait_ge(S["sel_ready"], 1)
            nc.scalar.activation(sel[:], sel[:], ACT.Exp).then_inc(S["exp_ready"], 1)
            for j in range(UP_BEFORE_EXP, UP):
                gelu(0, j)
            for h in range(2):
                act.wait_ge(S["cwT_mm"], h + 1)
                nc.scalar.activation(cwT[:, h * 512:(h + 1) * 512], bank[5 + h][0:NE, :], ACT.Copy)\
                    .then_inc(S["cwT_sb"], 1)
            for j in range(UP):
                gelu(1, j)

        @block.tensor
        def _(pe):
            mm = nc.tensor.matmul
            pe.wait_ge(in_qr, 48)
            mm(bank[0][0:D, 0:D], P_m[:], P_m[:], start=True, stop=False)
            mm(bank[0][0:D, 0:D], P_r[:], P_r[:], start=False, stop=True).then_inc(S["gram_ready"], 1)
            def product(dst, left, right, pairs=range(4)):
                for n, p in enumerate(pairs):
                    last = mm(dst[:, n * D:(n + 1) * D], left[:, p, :], right[:, p, :], start=True, stop=True)
                return last

            def beside_elimination():
                yield
                pe.wait_ge(silu_done, 2)
                pe.wait_ge(in_ada, 32)
                for n, ch in enumerate((0, 1, 3, 4)):
                    dst = bank[5][:, n * B:(n + 1) * B]
                    mm(dst, ada_m[:, ch * C:ch * C + P], s_m[:], start=True, stop=False)
                    last = mm(dst, ada_r[:, ch * C:ch * C + P], s_r[:], start=False, stop=True)
                last.then_inc(S["mod_mm"], 1)
                yield
                gm = ada_m[:].rearrange("p (g k c) -> p g k c", g=2, k=3)[:, :, 2, :]
                gr = ada_r[:].rearrange("p (g k c) -> p g k c", g=2, k=3)[:, :, 2, :]
                am = ada_m[:].rearrange("p (g c) -> p g c", g=6)[:, :, P:C]
                ar = ada_r[:].rearrange("p (g c) -> p g c", g=6)[:, :, P:C]
                for lo, m, rest in ((0, gm, gr), (2 * C, am, ar)):
                    dst = bank[4][0:B, lo:lo + (2 * C if lo == 0 else 6 * R)]
                    mm(dst, s_m[:], m, start=True, stop=False)
                    if lo == 0:
                        yield
                    last = mm(dst, s_r[:], rest, start=False, stop=True)
                last.then_inc(S["gate_mm"], 1)
                yield
                pe.wait_ge(in_rot, 32)
                pe.wait_ge(silu_done, 3)
                for j in range(D // 2):
                    g = j // 8
                    if j % 8 == 0:
                        mm(bank[2][:, 8 * g * B:8 * (g + 1) * B], rot_r[:, g, :], s_diag[:], start=True, stop=False)
                    last = mm(bank[2][:, j * B:(j + 1) * B], rot_m[:, j, :], s_m[:], start=False, stop=(j % 8 == 7))
                    if j % 4 == 3:
                        if j == D // 2 - 1:
                            last.then_inc(S["ent_ready"], 1)
                        yield
                pe.wait_ge(in_x, 48)
                for h in range(2):
                    dst = bank[6 + h][0:D, :]
                    mm(dst, P_m[:], xT_m[:, h * 512:(h + 1) * 512], start=True, stop=False)
                    yield
                    mm(dst, P_r[:], xT_r[:, h * 512:(h + 1) * 512], start=False, stop=True)\
                        .then_inc(S["xp_ready"], 1)
                    yield
                yield from steps(16, 20)
                pe.wait_ge(S["a_diag"], 1)
                product(bank[3], A_diag, A).then_inc(S["n1_mm"], 1)
                yield
                pe.wait_ge(S["gate_sb"], 1)
                pe.wait_ge(S["n1_sb"], 1)
                product(bank[4], N1_diag, N1).then_inc(S["n2_mm"], 1)
                yield
                pe.wait_ge(S["n2_sb"], 1)
                product(bank[3], N1_diag, N2).then_inc(S["n3_mm"], 1)
                yield
                product(bank[4], N2_diag, N2).then_inc(S["n3_mm"], 1)
                yield from steps(23, 26)
                pe.wait_ge(S["n4_sb"], 1)
                pe.wait_ge(S["mod_sb"], 1)
                pe.wait_ge(S["hi_ready"], 2)
                product(bank[5], N4_diag, Chi)
                yield
                product(bank[5][:, 4 * D:8 * D], N4_diag, Dhi).then_inc(S["hi_mm"], 1)
                yield from steps(27, 29)
                pe.wait_ge(S["xp_sb"], 1)
                pe.wait_ge(S["cd_ready"], 2)
                product(bank[6], A_diag, Dlo).then_inc(S["ad_mm"], 1)
                yield
                for n in range(2 * NSQ):
                    yield
                    h = n % 2
                    pe.wait_ge(S["x_diag"], n + 1)
                    half = (2 * h, 2 * h + 1)
                    product(bank[3 + h], X_diag[:, 1], X[:, 0], half)
                    product(bank[3 + h][:, 2 * D:4 * D], X_diag[:, 0], X[:, 1], half).then_inc(S["sq_mm"], 1)

            def gram_row(k):
                pe.wait_ge(S["row_used"], k + 1)
                mm(bank[0][0:D, 0:D + 1], ident[0:D, k:k + 1].to_broadcast([D, D]), EL[:, k:k + D + 1],
                   start=True, stop=True).then_inc(S["row_ready"], 1)

            gram_row(0)
            beside = beside_elimination()
            for k in range(D):
                pe.wait_ge(S["top_used"], k + 1)
                mm(bank[1][0:D, 0:D - k], ident[0:D, k:k + 1].to_broadcast([D, D]), TOP[:, k:D],
                   start=True, stop=True).then_inc(S["top_ready"], 1)
                if k + 1 < D - 1:
                    gram_row(k + 1)
                    next(beside, None)
            next(beside, None)
            pe.wait_ge(S["ln_ready"], 1)
            nc.tensor.transpose(bank[0][0:D, 0:D], LN[:], id64).then_inc(S["linvT_ready"], 1)
            next(beside, None)
            pe.wait_ge(S["lT_ready"], 1)
            pe.wait_ge(S["xp_sb"], 2)
            for h in range(2):
                mm(bank[2][h * D:(h + 1) * D, :], LT[:], xPT[:, h * 512:(h + 1) * 512], start=True, stop=True)\
                    .then_inc(S["z_ready"], 1)
            mm(bank[1][0:D, 0:C], LT[:], PT[:], start=True, stop=True).then_inc(S["basis_ready"], 1)
            for _ in beside:
                pass
            pe.wait_ge(S["f_ready"], 1)
            pe.wait_ge(S["z_sb"], 1)
            for b in range(B):
                half = slice(D * (b // 4), D * (b // 4 + 1))
                last = mm(bank[4 + b // 4][0:D, (b % 4) * T:(b % 4 + 1) * T], X[half, 0, b % 4, :],
                          Z0T[half, (b % 4) * T:(b % 4 + 1) * T], start=True, stop=True)
                if b % 4 == 3:
                    last.then_inc(S["turn_ready"], 1)
            def delta(b):
                if b == 0:
                    pe.wait_ge(S["turned_ready"], 1)
                    pe.wait_ge(S["z_sb"], 2)
                if b == 4:
                    pe.wait_ge(S["turned_hi"], 1)
                if b >= 2:
                    pe.wait_ge(S["xr_used"], b - 1)
                mm(bank[b % 2][:, 0:C], rt(WT, b), U0T[:], start=True, stop=True).then_inc(S["delta_ready"], 1)

            def transposed(ln, h):
                u = 2 * ln + h
                pe.wait_ge(S["h_ready"], u + 1)
                lo = ((2, 0), (0, 3))[ln][h]
                for b in range(4):
                    nc.tensor.transpose(bank[lo][:, b * T:(b + 1) * T], H[:, 4 * h + b, 0:P], ident)
                pe.wait_ge(S["hs_ready"], u + 1)
                for b in range(4):
                    last = nc.tensor.transpose(bank[lo + 1][0:RK, b * T // 2:(b + 1) * T // 2].bitcast(BF16),
                                               HS[:, 4 * h + b, :], identb[:])
                last.then_inc(S["hT_mm"], 1)

            for b in range(6):
                delta(b)
            pe.wait_ge(S["identb_ready"], 1)
            transposed(0, 0)
            delta(6)
            delta(7)
            pe.wait_ge(in_moe, N_MOE)
            pe.wait_ge(S["wst_ready"], 2)
            for b in range(B):
                if b == 4:
                    pe.wait_ge(S["xr_used"], B)
                    transposed(0, 1)
                pe.wait_ge(S["hT_sb"], b // 4 + 1)
                if b >= 4:
                    pe.wait_ge(S["r1_ready"], b - 3)
                dst = bank[4 + b % 4][:, 0:3 * C]
                mm(dst, rt(HT, b), wqkv_m, start=True, stop=False)
                mm(dst, rt(HST, b), wqkv_s, start=False, stop=True).then_inc(S["qkv_mm"], 1)

            def stacks_transposed(b):
                pe.wait_ge(S["stack_ready"], 2 * b + 2)
                if b >= 1:
                    pe.wait_ge(S["qkT_sb"], 2 * b)
                for g in range(2):
                    for p in range(NH // 2):
                        last = nc.tensor.transpose(bank[g][:, p * T // 2:(p + 1) * T // 2].bitcast(BF16),
                                                   QKS[:, b, g, 2 * p:2 * p + 2, :].rearrange("p h c -> p (h c)"),
                                                   identb[:])
                last.then_inc(S["qkT_mm"], 1)

            def scores_a(b, g):
                i = 4 * b + g
                if i >= 2:
                    pe.wait_ge(S["mx_ready"], i - 1)
                for j in range(2):
                    last = mm(bank[2 + g % 2][:, 2 * j * T:2 * (j + 1) * T], QT[:, b % 2, 2 * g + j, :],
                              KT[:, b % 2, 2 * g + j, :, :].rearrange("p i k -> p (i k)"), start=True, stop=True)
                last.then_inc(S["scoreA"], 1)

            def scores_b(b, g):
                i = 4 * b + g
                if i >= 2:
                    pe.wait_ge(S["pr_ready"], i - 1)
                for j in range(4):
                    pair = 2 * g + j // 2
                    last = mm(bank[4 + g % 2][:, j * T:(j + 1) * T], KT[:, b % 2, pair, j % 2, :],
                              QT[:, b % 2, pair, :], start=True, stop=True)
                last.then_inc(S["scoreB"], 1)

            def weighted(b, g):
                pe.wait_ge(S["pr_ready"], 4 * b + g + 1)
                if b >= 1 and g == 0:
                    pe.wait_ge(S["oT_sb"], b)
                for j in range(4):
                    head = 4 * g + j
                    lo, col = VW * (head % 4), T * (head // 4)
                    last = mm(bank[6][lo:lo + VW, col:col + T], VA[:, b, head, :], PR[:, b % 2, 4 * g + j, :],
                              start=True, stop=True)
                if g == 3:
                    last.then_inc(S["pv_mm"], 1)

            def maxima_transposed(b):
                pe.wait_ge(S["ms_ready"], b + 1)
                if b >= 2:
                    pe.wait_ge(S["x2_ready"], b - 1)
                for p in range(NH // 2):
                    last = nc.tensor.transpose(bank[7][:, p * T // 2:(p + 1) * T // 2].bitcast(BF16),
                                               QKS[:, b, 0, 2 * p:2 * p + 2, :].rearrange("p h c -> p (h c)"),
                                               identb[:])
                last.then_inc(S["mxT_mm"], 1)

            def back(b):
                pe.wait_ge(S["os_sb"], b + 1)
                if b + 1 < B:
                    pe.wait_ge(S["mxT_sb"], b + 2)
                if b >= 1:
                    pe.wait_ge(S["x2_ready"], b)
                for j in range(4):
                    last = nc.tensor.transpose(bank[7][:, j * P:(j + 1) * P], OS[:, j, :], ident)
                last.then_inc(S["back_mm"], 1)

            def out_transposed(b):
                pe.wait_ge(S["o_ready"], b + 1)
                nc.tensor.transpose(bank[6][:, 0:T], OA[:, b % 2, 0:P], ident)
                nc.tensor.transpose(bank[6][0:R, T:2 * T], OA[:, b % 2, P:C], ident).then_inc(S["oT_mm"], 1)

            def projected(b):
                pe.wait_ge(S["oT_sb"], b + 1)
                if b + 1 < B:
                    pe.wait_ge(S["mxT_sb"], b + 2)
                mm(bank[7][:, 0:C], OT_m[:, b % 2, :], wp_m[:], start=True, stop=False)
                mm(bank[7][:, 0:C], OT_r[:, b % 2, :], wp_r[:], start=False, stop=True).then_inc(S["attn_mm"], 1)

            stacks_transposed(0)
            pe.wait_ge(S["qkT_sb"], 2)
            for g in range(4):
                scores_a(0, g)
            stacks_transposed(1)
            maxima_transposed(0)
            pe.wait_ge(S["qkT_sb"], 4)
            scores_a(1, 0)
            scores_a(1, 1)
            for b in range(B):
                pe.wait_ge(S["mxT_sb"], b + 1)
                scores_b(b, 0)
                scores_b(b, 1)
                if b >= 1:
                    out_transposed(b - 1)
                if b + 1 < B:
                    scores_a(b + 1, 2)
                if b >= 1:
                    projected(b - 1)
                weighted(b, 0)
                scores_b(b, 2)
                if b + 1 < B:
                    scores_a(b + 1, 3)
                else:
                    transposed(1, 0)
                weighted(b, 1)
                scores_b(b, 3)
                if b + 2 < B:
                    stacks_transposed(b + 2)
                if b + 1 < B:
                    maxima_transposed(b + 1)
                weighted(b, 2)
                weighted(b, 3)
                if b + 2 < B:
                    pe.wait_ge(S["qkT_sb"], 2 * b + 6)
                    scores_a(b + 2, 0)
                    scores_a(b + 2, 1)
                back(b)
            out_transposed(B - 1)
            projected(B - 1)

            def up(h, j):
                n = h * UP + j
                if n >= 3:
                    pe.wait_ge(S["act_ready"], n - 2)
                cols = slice(j * P, (j + 1) * P)
                dst = bank[n % 3][:, :]
                mm(dst, w1_m[:, cols], HT[:, h * HALF:(h + 1) * HALF], start=True, stop=False)
                mm(dst, w1_s[:, cols], HST[:, h * HALF:(h + 1) * HALF], start=False, stop=True)\
                    .then_inc(S["up_mm"], 1)

            def down(b):
                i = b % 4
                if b >= 2:
                    pe.wait_ge(S["down_used"], b - 1)
                for e in range(NE):
                    lo = bank[3 + 2 * (b % 2) + e % 2]
                    if e == 0:
                        mm(lo[:, 2 * C:3 * C], rt(cwT, b), b2_s[:], start=True, stop=True)
                    dst = lo[:, (e // 2) * C:(e // 2 + 1) * C]
                    first, end = e * HID, (e + 1) * HID
                    for t in range(first // P, -(-end // P)):
                        rows = slice(max(first - t * P, 0), min(end - t * P, P))
                        last = mm(dst, HM[rows, t, i * T:(i + 1) * T], w2_s[rows, t, :],
                                  start=(t == first // P), stop=(t == -(-end // P) - 1))
                last.then_inc(S["down_mm"], 1)

            pe.wait_ge(S["wst_ready"], N_ST // ST_COLS)
            pe.wait_ge(S["mx_ready"], 4 * B)
            pe.wait_ge(S["hT_sb"], 3)
            for j in range(UP_BEFORE_NORM):
                up(0, j)
            transposed(1, 1)
            for j in range(UP_BEFORE_NORM, UP_BEFORE_LOGITS):
                up(0, j)
            pe.wait_ge(S["hT_sb"], 4)
            pe.wait_ge(S["x2_ready"], B)
            for b in range(B):
                dst = bank[7][:, b * NE:(b + 1) * NE]
                mm(dst, rt(HT, b), wg_m, start=True, stop=False)
                last = mm(dst, rt(HST, b), wg_s, start=False, stop=True)
            last.then_inc(S["lg_mm"], 1)
            for j in range(UP_BEFORE_LOGITS, UP):
                up(0, j)
            pe.wait_ge(S["cw_ready"], 1)
            for h in range(2):
                for b in range(4 * h, 4 * h + 4):
                    last = nc.tensor.transpose(bank[5 + h][0:NE, (b % 4) * T:(b % 4 + 1) * T], cw[:, b, :], ident)
                last.then_inc(S["cwT_mm"], 1)
            pe.wait_ge(S["act_ready"], UP)
            pe.wait_ge(S["cwT_sb"], 2)
            for b in range(4):
                down(b)
            for j in range(UP):
                up(1, j)
            pe.wait_ge(S["act_ready"], 2 * UP)
            for b in range(4, B):
                down(b)

        count = [0]

        @block.vector
        def _(dve):
            V = nc.vector

            def start(ins):
                count[0] += 1
                ins.then_inc(dve_done, 1)
                return count[0]

            def seq(ins):
                dve.wait_ge(dve_done, start(ins))

            dve.wait_ge(in_cst, 16)
            V.tensor_copy(identb[:], ident).then_inc(S["identb_ready"], 1)

            def beside_elimination():
                yield from steps(0, 6)
                dve.wait_ge(S["mod_mm"], 1)
                at = start(V.tensor_copy(MOD[:], bank[5][:, 0:4 * B].rearrange("p (c b) -> p c b", c=4)))
                dve.wait_ge(S["gate_sb"], 1)
                sc = gates8[:, 2 * C:].rearrange("p (l k c) -> p l k c", l=2, k=3)[:, :, 1, :]
                V.tensor_scalar(sc, sc, 1.0, None, ALU.add).then_inc(S["gates_ready"], 2)
                dve.wait_ge(dve_done, at)
                sc = MOD[:].rearrange("p (l k) b -> p l k b", l=2)[:, :, 1, :]
                V.tensor_scalar(sc, sc, 1.0, None, ALU.add).then_inc(S["mod_sb"], 1)
                yield from steps(6, 14)
                dve.wait_ge(S["quad_in"], 32)
                dve.wait_ge(S["quad_sb"], 1)
                seq(V.tensor_tensor(A[:], A[:], rot_bias.unsqueeze(1).to_broadcast([P, 4, D]), ALU.add))
                at = start(V.tensor_tensor(A[:], A[:], skew_sign.unsqueeze(1).to_broadcast([P, 4, D]), ALU.mult))
                yield
                dve.wait_ge(dve_done, at)
                dve.wait_ge(S["diag_zeroed"], 1)
                for h in range(2):
                    half = slice(h * D, (h + 1) * D)
                    V.tensor_reduce(norms[half, 4 * h:4 * h + 4], A[half], AX_X, ALU.add,
                                    apply_absolute_value=True).then_inc(S["norms_ready"], 1)
                yield from steps(15, 17)
                dve.wait_ge(S["norm_ready"], 1)
                for h in range(2):
                    half = slice(h * D, (h + 1) * D)
                    at = start(V.tensor_copy(norm[half], norm8[half, 4 * h:4 * h + 4]))
                dve.wait_ge(dve_done, at)
                at = start(V.tensor_tensor(active[:], norm[:].unsqueeze(1).to_broadcast([P, NSQ, 4]),
                                           thresholds.unsqueeze(2).to_broadcast([P, NSQ, 4]), ALU.is_gt))
                yield
                dve.wait_ge(dve_done, at)
                seq(V.tensor_tensor(shrink[:], active[:].rearrange("p k b -> p b k"),
                                    halvings.unsqueeze(1).to_broadcast([P, 4, NSQ]), ALU.mult))
                seq(V.tensor_reduce(scale[:], shrink[:], AX_X, ALU.add))
                seq(V.tensor_scalar(scale[:], scale[:], -1.0, 1.0, ALU.mult, ALU.add))
                V.tensor_tensor(A[:], A[:], scale[:].unsqueeze(2).to_broadcast([P, 4, D]), ALU.mult)\
                    .then_inc(S["a_ready"], 1)
                yield from steps(18, 24)
                dve.wait_ge(S["n3_sb"], 4)
                idb = id_stacked.unsqueeze(1).to_broadcast([P, 4, D])
                for n, two in enumerate((((Chi, cosc[4:]), (Dhi, sinc[4:])), ((Clo, cosc[:4]), (Dlo, sinc[:4])))):
                    for power, term in ((2, N2), (1, N1), (0, idb)):
                        for p, c in two:
                            ins = V.scalar_tensor_tensor(p, term, c[power], p, ALU.mult, ALU.add)
                            if n == 0 and power == 0:
                                ins.then_inc(S["hi_ready"], 1)
                            else:
                                at = start(ins)
                        if power < 2:
                            yield
                        dve.wait_ge(dve_done, at)
                dve.wait_ge(S["hi_mm"], 1)
                V.tensor_tensor(Clo, bank[5][:, 0:4 * D].rearrange("p (b j) -> p b j", b=4), Clo, ALU.add)                    .then_inc(S["cd_ready"], 1)
                V.tensor_tensor(Dlo, bank[5][:, 4 * D:8 * D].rearrange("p (b j) -> p b j", b=4), Dlo, ALU.add)                    .then_inc(S["cd_ready"], 1)
                yield
                dve.wait_ge(S["cd_ready"], 2)
                dve.wait_ge(S["ad_mm"], 1)
                ad = bank[6][:, 0:4 * D].rearrange("p (b j) -> p b j", b=4)
                V.tensor_tensor(X[:, 1], ad, Clo, ALU.add).then_inc(S["x_ready"], 1)
                V.scalar_tensor_tensor(X[:, 0], ad, -1.0, Clo, ALU.mult, ALU.add).then_inc(S["x_ready"], 1)
                yield
                for n in range(2 * NSQ):
                    yield
                    h = n % 2
                    dve.wait_ge(S["sq_mm"], n + 1)
                    if n < 2:
                        dve.wait_ge(S["x_ready"], 2)
                    mask = active[:, n // 2, 2 * h:2 * h + 2].unsqueeze(1).unsqueeze(3).to_broadcast([P, 2, 2, D])
                    V.copy_predicated(X[:, :, 2 * h:2 * h + 2, :], mask.bitcast(I32),
                                      bank[3 + h][:, 0:4 * D].rearrange("p (e b j) -> p e b j", e=2, b=2))\
                        .then_inc(S["x_step"], 1)
                dve.wait_ge(S["x_step"], 2 * NSQ)
                V.tensor_tensor(X[:, 0], X[:, 0], idb, ALU.subtract).then_inc(S["f_ready"], 1)

            dve.wait_ge(S["gram_ready"], 1)
            V.tensor_scalar(TOP[:], PT[:, 0:D], 0.5, None, ALU.mult).then_inc(S["top_used"], 1)
            seq(V.tensor_copy(EL[:, 0:D], bank[0][0:D, 0:D]))
            V.tensor_copy(EL[:, D:2 * D], id64).then_inc(S["row_used"], 1)

            def pivot(k):
                dve.wait_ge(S["row_ready"], k + 1)
                V.reciprocal(rpiv[:, k % 2:k % 2 + 1], bank[0][0:D, 0:1]).then_inc(S["rpiv_ready"], 1)

            def gram_update(k):
                dve.wait_ge(S["coef_ready"], k + 1)
                if k:
                    dve.wait_ge(S["row_used"], k + 1)
                win = EL[:, k + 1:k + 1 + D]
                V.scalar_tensor_tensor(win, bank[0][0:D, 1:D + 1], coef[:, k % 2:k % 2 + 1], win,
                                       ALU.mult, ALU.add).then_inc(S["row_used"], 1)

            def top_scaled(k):
                dve.wait_ge(S["rnrm_ready"], k + 1)
                dve.wait_ge(S["top_used"], k + 1)
                start(V.tensor_tensor(scaled[:], TOP[:, k:k + 1], rnrm_below[:, k % 2:k % 2 + 1], ALU.mult))

            beside = beside_elimination()
            pivot(0)
            gram_update(0)
            top_scaled(0)
            for k in range(D):
                row = bank[1]
                col = slice(k % 2, k % 2 + 1)
                sign = SG[:, k:k + 1]
                dve.wait_ge(S["top_ready"], k + 1)
                signed = start(V.tensor_scalar(sign, row[0:D, 0:1], 0.0, -0.5, ALU.is_ge, ALU.add))
                if k == D - 1:
                    break
                over_norm = start(V.tensor_tensor(sized[:], row[0:D, 0:1], rnrm[:, col], ALU.mult))
                dve.wait_ge(dve_done, over_norm)
                led = start(V.tensor_tensor(lead[:], sized[:], sign, ALU.add))
                if k + 1 < D - 1:
                    pivot(k + 1)
                start(V.scalar_tensor_tensor(reflected[:], coef[:, col], sign, scaled[:], ALU.mult, ALU.add))
                dve.wait_ge(dve_done, led)
                inverted = start(V.reciprocal(rlead[:], lead[:]))
                dve.wait_ge(dve_done, inverted)
                weighed = start(V.tensor_tensor(tcoef[:], reflected[:], rlead[:], ALU.mult))
                dve.wait_ge(dve_done, weighed)
                V.scalar_tensor_tensor(TOP[:, k + 1:D], row[0:D, 1:D - k], tcoef[:], TOP[:, k + 1:D],
                                       ALU.mult, ALU.add).then_inc(S["top_used"], 1)
                if k + 1 < D - 1:
                    gram_update(k + 1)
                    top_scaled(k + 1)
                    next(beside, None)
                else:
                    dve.wait_ge(S["row_used"], D)
                    seq(V.tensor_tensor(diagonal[:], EL[:, 0:D], id64, ALU.mult))
                    V.tensor_reduce(piv[:], diagonal[:], AX_X, ALU.add).then_inc(S["piv_ready"], 1)
            dve.wait_ge(dve_done, signed)
            seq(V.tensor_tensor(sign_of[:], SG[:], id64, ALU.mult))
            seq(V.tensor_reduce(sigma[:], sign_of[:], AX_X, ALU.add))
            dve.wait_ge(S["rnorm_ready"], 1)
            seq(V.tensor_scalar(signed_rnorm[:], sigma[:], 2.0, rnorm[:], ALU.mult, ALU.mult))
            V.tensor_scalar(LN[:], EL[:, D:2 * D], signed_rnorm[:], None, ALU.mult).then_inc(S["ln_ready"], 1)
            next(beside, None)
            dve.wait_ge(S["linvT_ready"], 1)
            V.tensor_copy(LT[:], bank[0][0:D, 0:D]).then_inc(S["lT_ready"], 1)
            next(beside, None)
            dve.wait_ge(S["z_ready"], 2)
            V.tensor_copy(Z0T[:], bank[2][:, :]).then_inc(S["z_sb"], 1)
            dve.wait_ge(S["basis_ready"], 1)
            V.tensor_copy(U0T[:], bank[1][0:D, 0:C]).then_inc(S["z_sb"], 1)
            for _ in beside:
                pass
            dve.wait_ge(S["turn_ready"], 1)
            V.tensor_copy(WT[:, 0:HALF], bank[4][0:D, :]).then_inc(S["turned_ready"], 1)

            def norm_stats(src, ln, b):
                seq(V.bn_stats(stats[:, b, :], src))
                V.bn_aggr(mv[:, ln, b, :], stats[:, b, :]).then_inc(S["var_ready"], 1)

            def normalized(src, ln, h):
                u = 2 * ln + h
                dve.wait_ge(S["var_ready"], 4 * (u + 1))
                dve.wait_ge(S["rstd_ready"], u + 1)
                half = slice(4 * h, 4 * h + 4)
                for b in range(4 * h, 4 * h + 4):
                    ins = V.tensor_scalar(H[:, b, :], src[:, b, :], mv[:, ln, b, 0:1], rstd[:, ln, b:b + 1],
                                          ALU.subtract, ALU.mult)
                ins.then_inc(S["h_ready"], 1)
                dve.wait_ge(S["h_ready"], u + 1)
                stack = HS[:, half, 0:RS].rearrange("p b (s c) -> p b s c", s=SLOTS)
                seq(V.tensor_tensor(hr[:], H[:, half, P:C], MB[:, half, 3 * ln + 1, :], ALU.mult))
                seq(V.tensor_tensor(hr[:], hr[:], MB[:, half, 3 * ln, :], ALU.add))
                seq(V.tensor_copy(stack[:, :, 0:3, :], hr[:].unsqueeze(2).to_broadcast([P, 4, 3, R])))
                seq(V.tensor_tensor(hres[:], hr[:], stack[:, :, 0, :], ALU.subtract))
                seq(V.tensor_copy(stack[:, :, 3:6:2, :], hres[:].unsqueeze(2).to_broadcast([P, 4, 2, R])))
                seq(V.tensor_tensor(hr[:], hres[:], stack[:, :, 3, :], ALU.subtract))
                V.tensor_copy(stack[:, :, 4, :], hr[:]).then_inc(S["hs_ready"], 1)
                dve.wait_ge(S["hs_ready"], u + 1)

            def moved(b):
                dve.wait_ge(S["delta_ready"], b + 1)
                V.tensor_tensor(XR[:, b, :], bank[b % 2][:, 0:C], x_in[:, b, :], ALU.add).then_inc(S["xr_used"], 1)
                dve.wait_ge(S["xr_used"], b + 1)
                norm_stats(XR[:, b, :], 0, b)

            for b in range(4):
                moved(b)
            dve.wait_ge(S["zeroed"], 6)
            dve.wait_ge(gates_in, 32)
            moved(4)
            normalized(XR, 0, 0)
            for b in range(5, B):
                moved(b)
            normalized(XR, 0, 1)
            for b in range(B):
                dve.wait_ge(S["qk1_sb"], b + 1)
                qkv = bank[4 + b % 4]
                V.tensor_copy(VA[:, b, :, 0:HD], qkv[:, 2 * C:3 * C].rearrange("p (h d) -> p h d", h=NH))\
                    .then_inc(S["v_sb"], 1)
                V.tensor_tensor(qkres[:, b, :].rearrange("p (g d) -> p g d", d=HD),
                                qkv[:, 0:2 * C].rearrange("p (g d) -> p g d", d=HD),
                                QKS[:, b, :, :, 2 * HD:3 * HD].rearrange("p g h d -> p (g h) d"), ALU.subtract)\
                    .then_inc(S["r1_ready"], 1)

            def stacks_moved(b):
                dve.wait_ge(S["qkT_mm"], b + 1)
                if b >= 2:
                    dve.wait_ge(S["scoreB"], 4 * b - 4)
                V.tensor_copy(QT[:, b % 2].rearrange("p h q -> p (h q)"), bank[0][:, :].bitcast(BF16))\
                    .then_inc(S["qkT_sb"], 1)
                for i in range(2):
                    half = slice(i * HK, (i + 1) * HK)
                    ins = V.tensor_copy(KT[half, b % 2, :, i, :],
                                        bank[1][half, :].bitcast(BF16).rearrange("p (h k) -> p h k", h=NH // 2))
                ins.then_inc(S["qkT_sb"], 1)

            def maxima(b, groups):
                for g in groups:
                    dve.wait_ge(S["scoreA"], 4 * b + g + 1)
                    V.tensor_reduce(nmax[:, 4 * g:4 * g + 4], bank[2 + g % 2][:, :].rearrange("p (h k) -> p h k", h=4),
                                    AX_X, ALU.max, negate=True).then_inc(S["mx_ready"], 1)

            def maxima_stacked(b):
                dve.wait_ge(S["mx_ready"], 4 * b + 4)
                parts = QKS[:, b, 0, :, DK:DM]
                seq(V.tensor_copy(parts[:, :, 0], nmax[:]))
                seq(V.tensor_tensor(nmres[:], nmax[:], parts[:, :, 0], ALU.subtract))
                V.tensor_copy(parts[:, :, 1], nmres[:]).then_inc(S["ms_ready"], 1)
                dve.wait_ge(S["ms_ready"], b + 1)

            def divided(b):
                dve.wait_ge(S["back_mm"], b + 1)
                o = bank[7][:, :].rearrange("p (h d) -> p h d", h=NH)
                seq(V.reciprocal(rsum[:, b % 2, :], o[:, :, HD]))
                V.tensor_tensor(OA[:, b % 2, :].rearrange("p (h d) -> p h d", h=NH), o[:, :, 0:HD],
                                rsum[:, b % 2, :].unsqueeze(2).to_broadcast([P, NH, HD]), ALU.mult)\
                    .then_inc(S["o_ready"], 1)

            def added(b):
                dve.wait_ge(S["attn_mm"], b + 1)
                seq(V.tensor_tensor(PG[:, b % 2, :], bank[7][:, 0:C], GB[:, b, 0, :], ALU.mult))
                V.tensor_tensor(X2[:, b, :], PG[:, b % 2, :], XR[:, b, :], ALU.add).then_inc(S["x2_ready"], 1)
                dve.wait_ge(S["x2_ready"], b + 1)
                norm_stats(X2[:, b, :], 1, b)

            stacks_moved(0)
            maxima(0, range(4))
            maxima_stacked(0)
            stacks_moved(1)
            maxima(1, (0, 1))
            for b in range(B):
                if b + 1 < B:
                    maxima(b + 1, (2, 3))
                    maxima_stacked(b + 1)
                if b >= 1:
                    added(b - 1)
                if b + 2 < B:
                    stacks_moved(b + 2)
                    maxima(b + 2, (0, 1))
                divided(b)
                if b == B - 2:
                    normalized(X2, 1, 0)
            added(B - 1)
            normalized(X2, 1, 1)

            dve.wait_ge(S["lg_sb"], 1)
            other = lg[:].unsqueeze(2).to_broadcast([P, B, NE, NE])
            own = lg[:].unsqueeze(3).to_broadcast([P, B, NE, NE])
            seq(V.tensor_tensor(gt[:], other, own, ALU.is_gt))
            seq(V.tensor_tensor(eq[:], other, own, ALU.is_equal))
            ties = rank_ties.unsqueeze(1).to_broadcast([P, B, NE * NE])
            eqf = eq[:].rearrange("p b e f -> p b (e f)")
            seq(V.tensor_tensor(eqf, eqf, ties, ALU.mult))
            seq(V.tensor_tensor(gt[:], gt[:], eq[:], ALU.add))
            seq(V.tensor_reduce(rank[:], gt[:], AX_X, ALU.add))
            seq(V.tensor_scalar(rank[:], rank[:], 1.5, None, ALU.is_lt))
            seq(V.tensor_reduce(gmax[:], lg[:], AX_X, ALU.max))
            V.tensor_tensor(sel[:], lg[:], gmax[:].unsqueeze(2).to_broadcast([P, B, NE]), ALU.subtract)\
                .then_inc(S["sel_ready"], 1)
            dve.wait_ge(S["exp_ready"], 1)
            seq(V.tensor_tensor(sel[:], sel[:], rank[:], ALU.mult))
            seq(V.tensor_reduce(gsum[:], sel[:], AX_X, ALU.add))
            seq(V.reciprocal(rgs[:], gsum[:]))
            V.tensor_tensor(cw[:], sel[:], rgs[:].unsqueeze(2).to_broadcast([P, B, NE]), ALU.mult)\
                .then_inc(S["cw_ready"], 1)
            dve.wait_ge(S["cw_ready"], 1)
            for b in range(B):
                acc = ACC[:, b % 2, :]
                dve.wait_ge(S["down_mm"], b + 1)
                lo = 3 + 2 * (b % 2)
                seq(V.tensor_copy(acc, bank[lo][:, 2 * C:3 * C]))
                for e in range(NE):
                    src = bank[lo + e % 2][:, (e // 2) * C:(e // 2 + 1) * C]
                    ins = V.scalar_tensor_tensor(acc, src, cw[:, b, e:e + 1], acc, ALU.mult, ALU.add)
                    if e == NE - 1:
                        ins.then_inc(S["down_used"], 1)
                        dve.wait_ge(S["down_used"], b + 1)
                    else:
                        seq(ins)
                seq(V.tensor_tensor(acc, acc, GB[:, b, 1, :], ALU.mult))
                V.tensor_tensor(X2[:, b, :], acc, X2[:, b, :], ALU.add).then_inc(S["res_ready"], 1)


def _layout(inputs):
    import numpy as np
    f = {k: np.asarray(v) for k, v in inputs.items()}
    ones = lambda n: np.ones((1, n), np.float32)

    def with_bias(w, b):
        return np.ascontiguousarray(np.concatenate([w, b.reshape(1, -1)], 0))

    x = np.ascontiguousarray(f["x"])
    iu, ju = np.triu_indices(D, k=1)
    rot = np.zeros((C, D, D), np.float32)
    rot[:, ju, iu] = f["L0_cond_W"].T
    rot[:, iu, ju] = f["L0_cond_W"].T
    rot = rot.reshape(C, 2, D // 2, D).transpose(0, 2, 1, 3)
    cond_diag = np.zeros((8, R, 8, B), np.float32)
    for j in range(8):
        cond_diag[j, :, j] = f["cond_1152"].T[P:]
    cond_diag = cond_diag.reshape(P, 8 * B)
    rot_last = rot[P:].reshape(R, 4, 8, P).transpose(2, 0, 1, 3)
    bias_of = np.zeros((D, D), np.float32)
    bias_of[ju, iu] = f["L0_cond_b"]
    bias_of[iu, ju] = f["L0_cond_b"]
    qkv, w1 = f["L1_cond_w_qkv"], f["L1_cond_w1"].transpose(1, 0, 2).reshape(C, NE * HID)
    main = np.concatenate([qkv, f["L1_cond_w_gate"], w1], 1)
    bias = np.concatenate([f["L1_cond_b_qkv"], np.zeros(NE, np.float32), f["L1_cond_b1"].reshape(-1)])
    stack = np.concatenate([np.tile(main[P:C], (SLOTS, 1)), np.tile(bias[None], (3, 1))], 0)
    rows_of = np.repeat(np.array(WPART), R).tolist() + [1, 2, 3]
    c = np.zeros((P, 520), np.float32)
    c[:, 0:P] = np.eye(P)
    i = np.arange(D)
    c[0:D, 128:192] = 0.5 * np.eye(D)
    c[0:D, 192:256] = -(i[:, None] > i[None, :]).astype(np.float32)
    c[:, 256:320] = np.tile(np.sign(i[None, :] - i[:, None]), (2, 1))
    c[:, 392:456] = np.tile(np.eye(D), (2, 1))
    c[:, 456:520] = np.tile(bias_of, (2, 1))
    c[:, 320:320 + NSQ] = 2.0 ** (np.arange(NSQ) + 1)
    c[:, 340:340 + NSQ] = 2.0 ** -(np.arange(NSQ) + 1.0)
    e = np.arange(NE)
    c[:, 360:376] = (e[None, :] < e[:, None]).astype(np.float32).reshape(1, NE * NE)
    c[0:RK, 380] = [-1.0 if r >= 2 else 0.0 for r in rows_of]
    c[0:RK, 381] = [-1.0 if r == 3 else 0.0 for r in rows_of]
    return {
        "xtok": x, "xT": np.ascontiguousarray(x.reshape(B * T, C).T),
        "pmat": f["L0_cond_P"], "pT": np.ascontiguousarray(f["L0_cond_P"].T),
        "condT": np.concatenate([f["cond_1152"].T, ones(B)], 0),
        "rotW": rot[0:P].reshape(P, D * D), "condR": cond_diag, "rotR": rot_last.reshape(P, 4 * P),
        "adaW": with_bias(f["L1_cond_w_adaln"], f["L1_cond_b_adaln"]),
        "wproj": with_bias(f["L1_cond_w_proj"], f["L1_cond_b_proj"]),
        "wmain": main[0:P], "wstack": stack,
        "w2": f["L1_cond_w2"].reshape(NE * HID, C), "b2": f["L1_cond_b2"], "consts": c,
    }


def kernel(**inputs):
    import numpy as _np
    import concourse.bacc as _bacc
    from concourse import mybir as _mybir
    from concourse.bass_utils import run_bass_kernel_spmd as _run

    nc = _bacc.Bacc("TRN2", target_bir_lowering=False, num_devices=1)
    arrays, args = {}, {}
    for name, a in _layout(inputs).items():
        a = _np.ascontiguousarray(a)
        arrays[f"in_{name}"] = a
        args[name] = nc.dram_tensor(f"in_{name}", a.shape, _mybir.dt.from_np(a.dtype), kind="ExternalInput").ap()
    out = nc.dram_tensor("out", (B, T, C), _mybir.dt.from_np(_np.dtype("float32")), kind="ExternalOutput").ap()
    bass_conditional_rotation_moe_block(nc, out=out, **args)
    r = _run(nc, [arrays], core_ids=[0])
    return r.results[0]["out"]
```

```python
from contextlib import ExitStack

import concourse.bass as bass
from concourse import mybir

ALU = mybir.AluOpType
ACT = mybir.ActivationFunctionType
F32 = mybir.dt.float32
I32 = mybir.dt.int32
BF16 = mybir.dt.bfloat16
AX_X = mybir.AxisListType.X
RMAX = bass.bass_isa.ReduceOp.max

P = 128
B, T, C = 8, 128, 144
D = 64
NH, HD = 16, 9
NE, HID = 4, 576
R = C - P
RA = R + 1
NSQ = 18
NTERM = 8
SLOTS = 6
WPART = (3, 2, 1, 1, 1, 2)
RS = SLOTS * R
RK = RS + 3
HK = 64
DK = SLOTS * HD
DM = DK + 2
VW = 32
LN_EPS = 1e-6
QK_SCALE = float(HD) ** -0.5
UP = NE * HID // P
UP_BEFORE_NORM, UP_BEFORE_LOGITS = 5, 9
HALF = 4 * T
N_ST = 3 * C + NE + NE * HID
ST_COLS = N_ST // 10


def steps(now, then):
    return (None for _ in range(then - now))


def factorial(n):
    out = 1.0
    for i in range(2, n + 1):
        out *= i
    return out


def bass_conditional_rotation_moe_block(nc, xtok, xT, pmat, pT, condT, rotW, adaW, wmain, wproj, wstack,
                                        w2, b2, consts, rotR, condR, out):
    with ExitStack() as ctx:
        def sb(name, shape, dt=F32):
            return ctx.enter_context(nc.sbuf_tensor(name, shape, dt))

        def sem(name):
            return ctx.enter_context(nc.semaphore(name))

        bank = [ctx.enter_context(nc.psum_tensor(f"bank{i}", [P, 512], F32)) for i in range(8)]

        cst = sb("cst", [P, consts.shape[1]])
        ident = cst[:, 0:P]
        id64 = cst[0:D, 0:D]
        id_stacked = cst[:, 392:392 + D]
        rot_bias = cst[:, 456:456 + D]
        twice = cst[:, 520:520 + P]
        below = cst[0:D, 192:256]
        skew_sign = cst[:, 256:320]
        rank_ties = cst[:, 360:376]
        minus_23, minus_3 = cst[0:RK, 380:381], cst[0:RK, 381:382]
        identb = sb("identb", [P, P], BF16)
        P_m, P_r = sb("P_m", [P, D]), sb("P_r", [R, D])
        PT = sb("PT", [D, C])
        early = sb("early", [P, 2 * B * T])
        xT_m, xT_r = early[:, 0:B * T], early[0:R, B * T:2 * B * T]
        x_in = sb("x_in", [P, B, C])
        s_m, s_r = sb("s_m", [P, B]), sb("s_r", [RA, B])
        s_diag = sb("s_diag", [P, 8 * B])
        shared = sb("shared", [P, 12288])
        rot_m = shared[:, 0:D * D].rearrange("p (j o) -> p j o", j=D // 2)
        rot_r = shared[:, D * D:D * D + 4 * P].rearrange("p (g o) -> p g o", g=4)
        QKS = shared[:, 0:8192].bitcast(BF16).rearrange("p (b g h c) -> p b g h c", b=B, g=2, h=NH)
        PR = shared[:, 8192:12288].rearrange("p (s h q) -> p s h q", s=2, h=NH)
        HM = shared[:, 0:UP * HALF].rearrange("p (j n) -> p j n", j=UP)
        ada_m, ada_r = sb("ada_m", [P, 6 * C]), sb("ada_r", [RA, 6 * C])
        wm = sb("wm", [P, 3 * C + NE + NE * HID])
        wqkv_m, wg_m, w1_m = wm[:, 0:3 * C], wm[:, 3 * C:3 * C + NE], wm[:, 3 * C + NE:]
        wst32, wst = sb("wst32", [RK, N_ST]), sb("wst", [RK, N_ST], BF16)
        wqkv_s, wg_s, w1_s = wst[:, 0:3 * C], wst[:, 3 * C:3 * C + NE], wst[:, 3 * C + NE:]
        wp_m, wp_r = sb("wp_m", [P, C]), sb("wp_r", [RA, C])
        w2_s = sb("w2_s", [P, UP, C])
        b2_s = sb("b2_s", [NE, C])

        EL = sb("EL", [D, 2 * D])
        rpiv, coef = sb("rpiv", [D, 2]), sb("coef", [D, 2])
        rnrm, rnrm_below = sb("rnrm", [D, 2]), sb("rnrm_below", [D, 2])
        piv, rnorm = sb("piv", [D, 1]), sb("rnorm", [D, 1])
        mhalf = sb("mhalf", [P, B])
        LT = sb("LT", [D, D])
        xPT = sb("xPT", [D, B * T])
        U0T = sb("U0T", [D, C])
        Z0T = sb("Z0T", [P, HALF])
        TOP = sb("TOP", [D, D])
        SG = sb("SG", [D, D])
        sized, lead, rlead = sb("sized", [D, 1]), sb("lead", [D, 1]), sb("rlead", [D, 1])
        scaled, reflected, tcoef = sb("scaled", [D, 1]), sb("reflected", [D, 1]), sb("tcoef", [D, 1])
        diagonal, sign_of = sb("diagonal", [D, D]), sb("sign_of", [D, D])
        sigma, signed_rnorm = sb("sigma", [D, 1]), sb("signed_rnorm", [D, 1])
        LN = sb("LN", [D, D])

        A = sb("A", [P, 4, D])
        quadrant = sb("quadrant", [P, 4, D // 2])
        series = sb("series", [P, B * NH * VW])
        A_diag, N1_diag, N2_diag, N4_diag = (series[:, i * 4 * P:(i + 1) * 4 * P].rearrange("p (b j) -> p b j", b=4)
                                             for i in range(4))
        N1, N2, Chi, Dhi, Clo, Dlo = (series[:, 16 * P + i * 4 * D:16 * P + (i + 1) * 4 * D]
                                      .rearrange("p (b j) -> p b j", b=4) for i in range(6))
        X, X_diag = sb("X", [P, 2, 4, D]), sb("X_diag", [P, 2, 4, P])
        WT = sb("WT", [D, B * T])

        MOD = sb("MOD", [P, 4, B])
        gate_rows = nc.dram_tensor("gate_rows", (B, 2 * C + 6 * R), F32).ap()
        gates8 = sb("gates8", [B, 2 * C + 6 * R])
        GM = sb("GM", [P, B, 2 * C + 6 * R])
        GB = GM[:, :, 0:2 * C].rearrange("p b (g c) -> p b g c", g=2)
        MB = GM[:, :, 2 * C:].rearrange("p b (g c) -> p b g c", g=6)
        XR = sb("XR", [P, B, C])
        stats = sb("stats", [P, B, 6])
        mv = sb("mv", [P, 2, B, 2])
        veps, rstd = sb("veps", [P, 2, B]), sb("rstd", [P, 2, B])
        H = sb("H", [P, B, C])
        hr, hres = sb("hr", [P, 4, R]), sb("hres", [P, 4, R])
        HS = sb("HS", [P, B, RK], BF16)
        HT = sb("HT", [P, B * T])
        HST = sb("HST", [RK, B * T], BF16)
        qkres = sb("qkres", [P, B, 2 * C])
        qkres2 = sb("qkres2", [P, 2, 2 * C])
        QT = sb("QT", [P, 2, NH // 2, T], BF16)
        KT = early[:, :].bitcast(BF16).rearrange("p (s h i k) -> p s h i k", s=2, h=NH // 2, i=2)
        VA = series[:, :].rearrange("p (b h d) -> p b h d", b=B, h=NH)
        nmax, nmres = sb("nmax", [P, NH]), sb("nmres", [P, NH])
        OS = sb("OS", [P, 4, T])
        rsum = sb("rsum", [P, 2, NH])
        OA = sb("OA", [P, 2, C])
        OT_m, OT_r = sb("OT_m", [P, 2, T]), sb("OT_r", [RA, 2, T])
        PG = sb("PG", [P, 2, C])
        X2 = sb("X2", [P, B, C])
        lg = sb("lg", [P, B, NE])
        gt, eq = sb("gt", [P, B, NE, NE]), sb("eq", [P, B, NE, NE])
        rank = sb("rank", [P, B, NE])
        gmax = sb("gmax", [P, B])
        gsum, rgs = sb("gsum", [P, B]), sb("rgs", [P, B])
        sel = sb("sel", [P, B, NE])
        cw = sb("cw", [P, B, NE])
        cwT = xPT[0:NE, :]
        ACC = sb("ACC", [P, 2, C])

        in_cst, in_qr, in_cond, in_rot, in_x, in_ada, in_wst, in_weights, gates_in = (sem(n) for n in (
            "in_cst", "in_qr", "in_cond", "in_rot", "in_x", "in_ada", "in_wst", "in_weights", "gates_in"))
        dve_done = sem("dve_done")
        pool_done = sem("pool_done")
        silu_done = sem("silu_done")
        names = (
            "gram_ready ln_ready z_sb row_ready row_used rpiv_ready coef_ready rnrm_step rnrm_ready "
            "linvT_ready lT_ready basis_ready top_ready top_used a_ready a_diag ent_ready staged quad_sb "
            "quad_in n1_mm n1_sb n2_mm n2_sb n3_mm n3_sb n4_sb hi_ready hi_mm cd_ready ad_mm x_ready "
            "squared turned_back x_diag sq_mm sqi_mm diag_zeroed gates_ready piv_ready rnorm_ready xp_ready "
            "xp_sb z_ready turn_ready turned_ready turned_hi delta_ready zeroed xr_used var_ready "
            "rstd_ready h_ready hs_ready hT_mm hT_sb mod_mm mod_sb gate_mm gate_sb identb_ready wst_step "
            "wst_ready qkv_mm qk1_sb r1_ready pool_step stack_ready qkT_mm qT_sb kT_sb scoreA mx_ready "
            "ms_ready mxT_mm mxT_sb scoreB pr_ready pv_mm os_sb back_mm o_ready oT_mm oT_sb attn_mm "
            "x2_ready lg_mm lg_sb sel_ready exp_ready cw_ready cwT_mm cwT_sb up_mm act_ready down_mm "
            "down_used res_ready stored ").split()
        S = {n: sem(n) for n in names}

        cosc = [(-1.0) ** i / factorial(2 * i) for i in range(NTERM)]
        sinc = [(-1.0) ** i / factorial(2 * i + 1) for i in range(NTERM)]

        block = ctx.enter_context(nc.Block())

        def rt(ap, b):
            return ap[:, b * T:(b + 1) * T]

        @block.sync
        def _(sp):
            sp.dma_start(cst[:], consts).then_inc(in_cst, 16)
            sp.dma_start(P_m[:], pmat[0:P, :]).then_inc(in_qr, 16)
            sp.dma_start(P_r[:], pmat[P:C, :]).then_inc(in_qr, 16)
            sp.dma_start(PT[:], pT).then_inc(in_qr, 16)
            sp.dma_start(s_m[:], condT[0:P, :]).then_inc(in_cond, 16)
            sp.dma_start(s_r[:], condT[P:C + 1, :]).then_inc(in_cond, 16)
            sp.dma_start(s_diag[:], condR).then_inc(in_cond, 16)
            sp.dma_start(shared[:, 0:D * D], rotW).then_inc(in_rot, 16)
            sp.dma_start(shared[:, D * D:D * D + 4 * P], rotR).then_inc(in_rot, 16)
            sp.dma_start(xT_m, xT[0:P, :]).then_inc(in_x, 16)
            sp.dma_start(xT_r, xT[P:C, :]).then_inc(in_x, 16)
            sp.dma_start(ada_m[:], adaW[0:P, :]).then_inc(in_ada, 16)
            sp.dma_start(ada_r[:], adaW[P:C + 1, :]).then_inc(in_ada, 16)
            sp.dma_start(x_in[:], xtok.rearrange("b t c -> t b c")).then_inc(in_x, 16)
            sp.dma_start(wst32[:], wstack).then_inc(in_wst, 16)
            sp.dma_start(wp_m[:], wproj[0:P, :]).then_inc(in_weights, 16)
            sp.dma_start(wp_r[:], wproj[P:C + 1, :]).then_inc(in_weights, 16)
            sp.dma_start(wm[:], wmain).then_inc(in_weights, 16)
            sp.dma_start(w2_s[:], w2.rearrange("(t p) c -> p t c", p=P))\
                .then_inc(in_weights, 16)
            sp.dma_start(b2_s[:], b2).then_inc(in_weights, 16)
            sp.wait_ge(S["staged"], 2)
            sp.dma_start(A[D:P, :, 0:D // 2], quadrant[0:D, :, :]).then_inc(S["quad_in"], 16)
            sp.dma_start(A[0:D, :, D // 2:D], quadrant[D:P, :, :]).then_inc(S["quad_in"], 16)
            sp.wait_ge(S["gates_ready"], 2)
            sp.dma_start(gate_rows, gates8[:]).then_inc(gates_in, 16)
            sp.wait_ge(gates_in, 16)
            sp.dma_start(GM[:], gate_rows.unsqueeze(0).to_broadcast([P, B, 2 * C + 6 * R])).then_inc(gates_in, 16)
            for b in range(B):
                sp.wait_ge(S["res_ready"], b + 1)
                sp.dma_start(out[b], X2[:, b, :]).then_inc(S["stored"], 16)
            sp.wait_ge(S["stored"], 16 * B)
        WEIGHTS_IN = 16 * 5

        @block.gpsimd
        def _(pool):
            nc.gpsimd.memset(mhalf[:], -0.5).then_inc(pool_done, 1)
            nc.gpsimd.memset(X_diag[:].rearrange("p e b j -> p (e b j)"), 0.0).then_inc(S["diag_zeroed"], 1)
            nc.gpsimd.memset(series[:, 0:16 * P], 0.0).then_inc(S["diag_zeroed"], 1)

            def beside_elimination():
                yield
                nc.gpsimd.memset(HS[:], 1.0).then_inc(S["zeroed"], 1)
                yield
                nc.gpsimd.memset(OT_r[:], 1.0).then_inc(S["zeroed"], 1)
                yield from steps(2, 16)
                for h in range(2):
                    pool.wait_ge(S["xp_ready"], 2)
                    nc.gpsimd.memset(early[:, h * B * T:(h + 1) * B * T], 0.0).then_inc(S["zeroed"], 1)
                    yield
                pool.wait_ge(in_cst, 16)
                pool.wait_ge(in_wst, 16)
                n = 0
                for c in range(0, N_ST, ST_COLS):
                    part, whole = wst[:, c:c + ST_COLS], wst32[:, c:c + ST_COLS]
                    for minus in (minus_23, minus_3):
                        yield
                        nc.gpsimd.tensor_copy(part, whole).then_inc(S["wst_step"], 1)
                        yield
                        pool.wait_ge(S["wst_step"], n + 1)
                        nc.gpsimd.tensor_scalar(part, part, minus, None, ALU.mult).then_inc(S["wst_step"], 1)
                        yield
                        pool.wait_ge(S["wst_step"], n + 2)
                        nc.gpsimd.tensor_tensor(whole, whole, part, ALU.add).then_inc(S["wst_step"], 1)
                        n += 3
                        pool.wait_ge(S["wst_step"], n)
                    yield
                    nc.gpsimd.tensor_copy(part, whole).then_inc(S["wst_ready"], 1)

            beside = beside_elimination()
            for k in range(D - 1):
                pool.wait_ge(S["rpiv_ready"], k + 1)
                pool.wait_ge(S["row_used"], k + 1)
                nc.gpsimd.tensor_scalar(coef[:, k % 2:k % 2 + 1], EL[:, k:k + 1], rpiv[:, k % 2:k % 2 + 1],
                                        below[:, k:k + 1], ALU.mult, ALU.mult).then_inc(S["coef_ready"], 1)
                next(beside, None)
            pool.wait_ge(S["piv_ready"], 1)
            pool.wait_ge(pool_done, 1)
            nc.gpsimd.tensor_tensor(rnorm[:], piv[:], mhalf[0:D, 0:1], ALU.pow).then_inc(S["rnorm_ready"], 1)
            pool.wait_ge(S["ent_ready"], 1)
            nc.gpsimd.memset(QKS[:, :, :, :, DK:HK].rearrange("p b g h c -> p (b g h) c"), 0.0)\
                .then_inc(pool_done, 1)
            pool.wait_ge(pool_done, 2)
            nc.gpsimd.memset(QKS[:, :, 1, :, DK:DM], 1.0).then_inc(S["zeroed"], 1)
            pool.wait_ge(S["x_ready"], 2)
            nc.gpsimd.memset(series[:, :], 0.0).then_inc(pool_done, 1)
            pool.wait_ge(pool_done, 3)
            nc.gpsimd.memset(VA[:, :, :, HD:HD + 1], 1.0).then_inc(S["zeroed"], 1)

            def inverse_deviations(ln, h):
                u = 2 * ln + h
                pool.wait_ge(S["var_ready"], 4 * (u + 1))
                nc.gpsimd.tensor_scalar(veps[:, ln, 4 * h:4 * h + 4], mv[:, ln, 4 * h:4 * h + 4, 1], LN_EPS, None,
                                        ALU.add).then_inc(pool_done, 1)
                pool.wait_ge(pool_done, 4 + u)
                nc.gpsimd.tensor_tensor(rstd[:, ln, 4 * h:4 * h + 4], veps[:, ln, 4 * h:4 * h + 4], mhalf[:, 0:4],
                                        ALU.pow).then_inc(S["rstd_ready"], 1)

            inverse_deviations(0, 0)
            inverse_deviations(0, 1)
            for b in range(B):
                pool.wait_ge(S["r1_ready"], b + 1)
                stacks = QKS[:, b]
                res = qkres[:, b, :].rearrange("p (g h d) -> p g h d", g=2, h=NH)

                def slots(g, first, stride, n, stacks=stacks):
                    end = first + stride * (n - 1) + 1
                    parts = stacks[:, g, :, 0:DK].rearrange("p h (s d) -> p h s d", s=SLOTS)
                    return parts[:, :, first:end:stride, :]

                def wide(x, g, n):
                    return x[:, g].unsqueeze(2).to_broadcast([P, NH, n, HD])

                nc.gpsimd.tensor_copy(slots(0, 3, 2, 2), wide(res, 0, 2)).then_inc(S["pool_step"], 1)
                nc.gpsimd.tensor_copy(slots(1, 1, 4, 2), wide(res, 1, 2)).then_inc(S["pool_step"], 1)
                pool.wait_ge(S["pool_step"], 3 * b + 2)
                part2 = QKS[:, b, :, :, 5 * HD:6 * HD].rearrange("p g h d -> p (g h) d")
                r32 = qkres[:, b, :].rearrange("p (g d) -> p g d", d=HD)
                res2 = qkres2[:, b % 2, :].rearrange("p (g d) -> p g d", d=HD)
                nc.gpsimd.tensor_tensor(res2, r32, part2, ALU.subtract).then_inc(S["pool_step"], 1)
                pool.wait_ge(S["pool_step"], 3 * b + 3)
                res2 = qkres2[:, b % 2, :].rearrange("p (g h d) -> p g h d", g=2, h=NH)
                nc.gpsimd.tensor_copy(QKS[:, b, 0, :, 4 * HD:5 * HD], res2[:, 0]).then_inc(S["stack_ready"], 1)
                nc.gpsimd.tensor_copy(QKS[:, b, 1, :, 0:HD], res2[:, 1]).then_inc(S["stack_ready"], 1)
            for _ in beside:
                pass
            inverse_deviations(1, 0)
            inverse_deviations(1, 1)

        @block.scalar
        def _(act):
            act.wait_ge(in_cond, 48)
            nc.scalar.activation(s_m[:], s_m[:], ACT.Silu).then_inc(silu_done, 1)
            nc.scalar.activation(s_r[0:R, :], s_r[0:R, :], ACT.Silu).then_inc(silu_done, 1)
            nc.scalar.activation(s_diag[:], s_diag[:], ACT.Silu).then_inc(silu_done, 1)

            def diagonal_blocks(dst, src):
                nc.scalar.activation(dst[0:D, ..., 0:D], src[0:D], ACT.Copy)
                return nc.scalar.activation(dst[D:P, ..., D:P], src[D:P], ACT.Copy)

            def pairs(src):
                return src.rearrange("p (b j) -> p b j", b=4)

            def beside_elimination():
                yield from steps(0, 11)
                act.wait_ge(S["ent_ready"], 1)
                ent = bank[2][:, 0:D // 2 * B].rearrange("p (j h b) -> p h b j", h=2, b=4)
                nc.scalar.activation(quadrant[0:D], ent[0:D, 1], ACT.Copy).then_inc(S["staged"], 1)
                nc.scalar.activation(quadrant[D:P], ent[D:P, 0], ACT.Copy).then_inc(S["staged"], 1)
                nc.scalar.activation(A[0:D, :, 0:D // 2], ent[0:D, 0], ACT.Copy)
                nc.scalar.activation(A[D:P, :, D // 2:D], ent[D:P, 1], ACT.Copy).then_inc(S["quad_sb"], 1)
                def moved(h):
                    act.wait_ge(S["xp_ready"], h + 1)
                    nc.scalar.activation(xPT[:, h * 512:(h + 1) * 512], bank[6 + h][0:D, :], ACT.Copy)\
                        .then_inc(S["xp_sb"], 1)

                yield from steps(11, 13)
                moved(0)
                yield
                act.wait_ge(S["diag_zeroed"], 2)
                act.wait_ge(S["a_ready"], 1)
                diagonal_blocks(A_diag, A).then_inc(S["a_diag"], 1)
                yield
                moved(1)
                yield
                act.wait_ge(S["n1_mm"], 1)
                diagonal_blocks(N1_diag, pairs(bank[3][:, 0:4 * D]))
                nc.scalar.activation(N1, pairs(bank[3][:, 0:4 * D]), ACT.Copy).then_inc(S["n1_sb"], 1)
                yield
                act.wait_ge(S["n2_mm"], 1)
                diagonal_blocks(N2_diag, pairs(bank[4][:, 0:4 * D]))
                nc.scalar.activation(N2, pairs(bank[4][:, 0:4 * D]), ACT.Copy).then_inc(S["n2_sb"], 1)
                yield
                act.wait_ge(S["n3_mm"], 1)
                for p, c in ((Chi, cosc[7]), (Dhi, sinc[7]), (Clo, cosc[3]), (Dlo, sinc[3])):
                    nc.scalar.activation(p, pairs(bank[3][:, 0:4 * D]), ACT.Copy, scale=c).then_inc(S["n3_sb"], 1)
                yield
                act.wait_ge(S["n3_mm"], 2)
                diagonal_blocks(N4_diag, pairs(bank[4][:, 0:4 * D])).then_inc(S["n4_sb"], 1)
                yield from steps(19, 24)
                act.wait_ge(S["gate_mm"], 1)
                nc.scalar.activation(gates8[:], bank[7][0:B, 0:2 * C + 6 * R], ACT.Copy).then_inc(S["gate_sb"], 1)
                yield
                act.wait_ge(S["x_ready"], 2)
                for h in range(2):
                    diagonal_blocks(X_diag[:, :, 2 * h:2 * h + 2, :], X[:, :, 2 * h:2 * h + 2, :])\
                        .then_inc(S["x_diag"], 1)
                yield from steps(25, 27)
                for n in range(2 * (NSQ - 1)):
                    h = n % 2
                    act.wait_ge(S["sqi_mm"], n + 1)
                    nc.scalar.activation(X_diag[:, 1, 2 * h:2 * h + 2, :],
                                         bank[5 + h][:, 0:2 * P].rearrange("p (b j) -> p b j", b=2), ACT.Copy)\
                        .then_inc(S["turned_back"], 1)
                    yield

            beside = beside_elimination()
            for k in range(D - 1):
                act.wait_ge(S["rpiv_ready"], k + 1)
                col = slice(k % 2, k % 2 + 1)
                nc.scalar.activation(rnrm[:, col], rpiv[:, col], ACT.Sqrt).then_inc(S["rnrm_step"], 1)
                act.wait_ge(S["rnrm_step"], k + 1)
                nc.scalar.activation(rnrm_below[:, col], below[:, k:k + 1], ACT.Copy, scale=rnrm[:, col])\
                    .then_inc(S["rnrm_ready"], 1)
                next(beside, None)
            for _ in beside:
                pass
            act.wait_ge(S["turn_ready"], 2)
            nc.scalar.activation(WT[:, HALF:2 * HALF], bank[5][0:D, :], ACT.Copy).then_inc(S["turned_hi"], 1)

            def modulated(ln, h):
                u = 2 * ln + h
                act.wait_ge(S["hT_mm"], u + 1)
                lo = ((2, 0), (0, 3))[ln][h]
                for b in range(4):
                    nc.scalar.activation(rt(HT, 4 * h + b), bank[lo][:, b * T:(b + 1) * T], ACT.Identity,
                                         bias=MOD[:, 2 * ln, 4 * h + b:4 * h + b + 1],
                                         scale=MOD[:, 2 * ln + 1, 4 * h + b:4 * h + b + 1])
                nc.scalar.activation(HST[:, h * HALF:(h + 1) * HALF], bank[lo + 1][0:RK, 0:HALF // 2].bitcast(BF16),
                                     ACT.Copy).then_inc(S["hT_sb"], 1)

            act.wait_ge(S["mod_sb"], 1)
            modulated(0, 0)
            act.wait_ge(S["zeroed"], 6)
            for b in range(B):
                if b == 4:
                    modulated(0, 1)
                act.wait_ge(S["qkv_mm"], b + 1)
                qkv = bank[4 + b % 4][:, 0:2 * C].rearrange("p (g h d) -> p g h d", g=2, h=NH)
                for g, first in ((0, 0), (1, 2)):
                    dst = QKS[:, b, g, :, first * HD:(first + 3) * HD].rearrange("p h (s d) -> p h s d", s=3)
                    last = nc.scalar.activation(dst, qkv[:, g].unsqueeze(2).to_broadcast([P, NH, 3, HD]), ACT.Copy)
                last.then_inc(S["qk1_sb"], 1)

            def out_transposed(b):
                act.wait_ge(S["oT_mm"], b + 1)
                if b >= 2:
                    act.wait_ge(S["attn_mm"], b - 1)
                nc.scalar.activation(OT_m[:, b % 2, :], bank[6][:, 0:T], ACT.Copy)
                nc.scalar.activation(OT_r[0:R, b % 2, :], bank[6][0:R, T:2 * T], ACT.Copy).then_inc(S["oT_sb"], 1)

            def shifted(b):
                act.wait_ge(S["mxT_mm"], b + 1)
                nc.scalar.activation(QT[:, b % 2, :, :].rearrange("p h q -> p (h q)"),
                                     bank[7][:, :].bitcast(BF16), ACT.Copy).then_inc(S["mxT_sb"], 1)

            def queries_moved(b):
                act.wait_ge(S["qkT_mm"], b + 1)
                if b >= 2:
                    act.wait_ge(S["scoreB"], 4 * b - 4)
                nc.scalar.activation(QT[:, b % 2, :, :].rearrange("p h q -> p (h q)"),
                                     bank[0][:, :].bitcast(BF16), ACT.Copy).then_inc(S["qT_sb"], 1)

            queries_moved(0)
            queries_moved(1)
            shifted(0)
            for b in range(B):
                for g in range(4):
                    act.wait_ge(S["scoreB"], b * 4 + g + 1)
                    if b >= 2 and g == 0:
                        act.wait_ge(S["pv_mm"], b - 1)
                    nc.scalar.activation(PR[:, b % 2, 4 * g:4 * g + 4, :],
                                         bank[4 + g % 2][:, :].rearrange("p (h q) -> p h q", h=4),
                                         ACT.Exp, scale=QK_SCALE).then_inc(S["pr_ready"], 1)
                    if g == 0 and b >= 1:
                        out_transposed(b - 1)
                if b + 2 < B:
                    queries_moved(b + 2)
                if b + 1 < B:
                    shifted(b + 1)
                act.wait_ge(S["pv_mm"], b + 1)
                if b >= 1:
                    act.wait_ge(S["back_mm"], b)
                nc.scalar.activation(OS[:].rearrange("p j q -> p (j q)"), bank[6][:, :], ACT.Copy)\
                    .then_inc(S["os_sb"], 1)
                if b == B - 1:
                    modulated(1, 0)
            out_transposed(B - 1)

            def gelu(h, j):
                n = h * UP + j
                act.wait_ge(S["up_mm"], n + 1)
                if h and j == 0:
                    act.wait_ge(S["down_mm"], 4)
                nc.scalar.activation(HM[:, j, :], bank[n % 3][:, :], ACT.Gelu_apprx_tanh)\
                    .then_inc(S["act_ready"], 1)

            for j in range(UP_BEFORE_NORM):
                gelu(0, j)
            modulated(1, 1)
            for j in range(UP_BEFORE_NORM, UP_BEFORE_LOGITS):
                gelu(0, j)
            act.wait_ge(S["lg_mm"], 1)
            nc.scalar.activation(lg[:], bank[7][:, 0:B * NE].rearrange("p (b e) -> p b e", b=B), ACT.Copy)\
                .then_inc(S["lg_sb"], 1)
            for j in range(UP_BEFORE_LOGITS, UP):
                gelu(0, j)
            act.wait_ge(S["sel_ready"], 1)
            nc.scalar.activation(sel[:], sel[:], ACT.Exp).then_inc(S["exp_ready"], 1)
            for h in range(2):
                act.wait_ge(S["cwT_mm"], h + 1)
                nc.scalar.activation(cwT[:, h * 512:(h + 1) * 512], bank[5 + h][0:NE, :], ACT.Copy)\
                    .then_inc(S["cwT_sb"], 1)
            for j in range(UP):
                gelu(1, j)

        @block.tensor
        def _(pe):
            mm = nc.tensor.matmul
            pe.wait_ge(in_qr, 48)
            mm(bank[0][0:D, 0:D], P_m[:], P_m[:], start=True, stop=False)
            mm(bank[0][0:D, 0:D], P_r[:], P_r[:], start=False, stop=True).then_inc(S["gram_ready"], 1)
            def product(dst, left, right, pairs=range(4)):
                for n, p in enumerate(pairs):
                    last = mm(dst[:, n * D:(n + 1) * D], left[:, p, :], right[:, p, :], start=True, stop=True)
                return last

            def beside_elimination():
                yield from steps(0, 3)
                pe.wait_ge(in_rot, 32)
                pe.wait_ge(silu_done, 3)
                for j in range(D // 2):
                    g = j // 8
                    if j % 8 == 0:
                        mm(bank[2][:, 8 * g * B:8 * (g + 1) * B], rot_r[:, g, :], s_diag[:], start=True, stop=False)
                    last = mm(bank[2][:, j * B:(j + 1) * B], rot_m[:, j, :], s_m[:], start=False, stop=(j % 8 == 7))
                    if j % 4 == 3:
                        if j == D // 2 - 1:
                            last.then_inc(S["ent_ready"], 1)
                        yield
                pe.wait_ge(in_x, 48)
                for h in range(2):
                    dst = bank[6 + h][0:D, :]
                    mm(dst, P_m[:], xT_m[:, h * 512:(h + 1) * 512], start=True, stop=False)
                    yield
                    mm(dst, P_r[:], xT_r[:, h * 512:(h + 1) * 512], start=False, stop=True)\
                        .then_inc(S["xp_ready"], 1)
                    yield
                pe.wait_ge(S["a_diag"], 1)
                product(bank[3], A_diag, A).then_inc(S["n1_mm"], 1)
                yield
                pe.wait_ge(S["n1_sb"], 1)
                product(bank[4], N1_diag, N1).then_inc(S["n2_mm"], 1)
                yield
                pe.wait_ge(S["n2_sb"], 1)
                product(bank[3], N1_diag, N2).then_inc(S["n3_mm"], 1)
                yield
                product(bank[4], N2_diag, N2).then_inc(S["n3_mm"], 1)
                yield
                pe.wait_ge(silu_done, 2)
                pe.wait_ge(in_ada, 32)
                for n, ch in enumerate((0, 1, 3, 4)):
                    dst = bank[2][:, n * B:(n + 1) * B]
                    mm(dst, ada_m[:, ch * C:ch * C + P], s_m[:], start=True, stop=False)
                    last = mm(dst, ada_r[:, ch * C:ch * C + P], s_r[:], start=False, stop=True)
                last.then_inc(S["mod_mm"], 1)
                yield from steps(19, 21)
                pe.wait_ge(S["n4_sb"], 1)
                pe.wait_ge(S["hi_ready"], 2)
                product(bank[5], N4_diag, Chi)
                yield
                product(bank[5][:, 4 * D:8 * D], N4_diag, Dhi).then_inc(S["hi_mm"], 1)
                yield
                pe.wait_ge(S["xp_sb"], 2)
                gm = ada_m[:].rearrange("p (g k c) -> p g k c", g=2, k=3)[:, :, 2, :]
                gr = ada_r[:].rearrange("p (g k c) -> p g k c", g=2, k=3)[:, :, 2, :]
                am = ada_m[:].rearrange("p (g c) -> p g c", g=6)[:, :, P:C]
                ar = ada_r[:].rearrange("p (g c) -> p g c", g=6)[:, :, P:C]
                for lo, m, rest in ((0, gm, gr), (2 * C, am, ar)):
                    dst = bank[7][0:B, lo:lo + (2 * C if lo == 0 else 6 * R)]
                    mm(dst, s_m[:], m, start=True, stop=False)
                    last = mm(dst, s_r[:], rest, start=False, stop=True)
                last.then_inc(S["gate_mm"], 1)
                yield
                pe.wait_ge(S["xp_sb"], 1)
                pe.wait_ge(S["cd_ready"], 2)
                product(bank[6], A_diag, Dlo).then_inc(S["ad_mm"], 1)
                yield
                for n in range(2 * NSQ):
                    yield
                    h = n % 2
                    half = (2 * h, 2 * h + 1)
                    if n < 2:
                        pe.wait_ge(S["x_diag"], n + 1)
                    else:
                        pe.wait_ge(S["squared"], n - 1)
                        pe.wait_ge(S["turned_back"], n - 1)
                    for m, p in enumerate(half):
                        last = mm(bank[3 + h][:, m * P:(m + 1) * P], X_diag[:, 1, p, :], X_diag[:, 0, p, :],
                                  start=True, stop=True)
                    last.then_inc(S["sq_mm"], 1)
                    if n >= 2 * (NSQ - 1):
                        continue
                    mm(bank[5 + h][:, 0:2 * P], twice, X_diag[:, 1, 2 * h:2 * h + 2, :].rearrange("p b j -> p (b j)"),
                       start=True, stop=False)
                    for m, p in enumerate(half):
                        last = mm(bank[5 + h][:, m * P:(m + 1) * P], X_diag[:, 0, p, :], X_diag[:, 1, p, :],
                                  start=False, stop=(m == 1))
                    last.then_inc(S["sqi_mm"], 1)

            def gram_row(k):
                pe.wait_ge(S["row_used"], k + 1)
                mm(bank[0][0:D, 0:D + 1], ident[0:D, k:k + 1].to_broadcast([D, D]), EL[:, k:k + D + 1],
                   start=True, stop=True).then_inc(S["row_ready"], 1)

            gram_row(0)
            beside = beside_elimination()
            for k in range(D):
                pe.wait_ge(S["top_used"], k + 1)
                mm(bank[1][0:D, 0:D - k], ident[0:D, k:k + 1].to_broadcast([D, D]), TOP[:, k:D],
                   start=True, stop=True).then_inc(S["top_ready"], 1)
                if k + 1 < D - 1:
                    gram_row(k + 1)
                    next(beside, None)
            next(beside, None)
            pe.wait_ge(S["ln_ready"], 1)
            nc.tensor.transpose(bank[0][0:D, 0:D], LN[:], id64).then_inc(S["linvT_ready"], 1)
            next(beside, None)
            pe.wait_ge(S["lT_ready"], 1)
            pe.wait_ge(S["xp_sb"], 2)
            for h in range(2):
                mm(bank[2][h * D:(h + 1) * D, :], LT[:], xPT[:, h * 512:(h + 1) * 512], start=True, stop=True)\
                    .then_inc(S["z_ready"], 1)
            mm(bank[1][0:D, 0:C], LT[:], PT[:], start=True, stop=True).then_inc(S["basis_ready"], 1)
            for _ in beside:
                pass
            pe.wait_ge(S["squared"], 2 * NSQ)
            pe.wait_ge(S["z_sb"], 1)
            for b in range(B):
                half = slice(D * (b // 4), D * (b // 4 + 1))
                last = mm(bank[4 + b // 4][0:D, (b % 4) * T:(b % 4 + 1) * T], X_diag[half, 0, b % 4, half],
                          Z0T[half, (b % 4) * T:(b % 4 + 1) * T], start=True, stop=True)
                if b % 4 == 3:
                    last.then_inc(S["turn_ready"], 1)
            def delta(b):
                if b == 0:
                    pe.wait_ge(S["turned_ready"], 1)
                    pe.wait_ge(S["z_sb"], 2)
                if b == 4:
                    pe.wait_ge(S["turned_hi"], 1)
                if b >= 2:
                    pe.wait_ge(S["xr_used"], b - 1)
                mm(bank[b % 2][:, 0:C], rt(WT, b), U0T[:], start=True, stop=True).then_inc(S["delta_ready"], 1)

            def transposed(ln, h):
                u = 2 * ln + h
                pe.wait_ge(S["h_ready"], u + 1)
                lo = ((2, 0), (0, 3))[ln][h]
                for b in range(4):
                    nc.tensor.transpose(bank[lo][:, b * T:(b + 1) * T], H[:, 4 * h + b, 0:P], ident)
                pe.wait_ge(S["hs_ready"], u + 1)
                for b in range(4):
                    last = nc.tensor.transpose(bank[lo + 1][0:RK, b * T // 2:(b + 1) * T // 2].bitcast(BF16),
                                               HS[:, 4 * h + b, :], identb[:])
                last.then_inc(S["hT_mm"], 1)

            for b in range(6):
                delta(b)
            pe.wait_ge(S["identb_ready"], 1)
            transposed(0, 0)
            delta(6)
            delta(7)
            pe.wait_ge(in_weights, WEIGHTS_IN)
            pe.wait_ge(S["wst_ready"], 2)
            for b in range(B):
                if b == 4:
                    pe.wait_ge(S["xr_used"], B)
                    transposed(0, 1)
                pe.wait_ge(S["hT_sb"], b // 4 + 1)
                if b >= 4:
                    pe.wait_ge(S["r1_ready"], b - 3)
                dst = bank[4 + b % 4][:, 0:3 * C]
                mm(dst, rt(HT, b), wqkv_m, start=True, stop=False)
                mm(dst, rt(HST, b), wqkv_s, start=False, stop=True).then_inc(S["qkv_mm"], 1)

            def stacks_transposed(b):
                pe.wait_ge(S["stack_ready"], 2 * b + 2)
                if b >= 1:
                    pe.wait_ge(S["qT_sb"], b)
                    pe.wait_ge(S["kT_sb"], b)
                for g in range(2):
                    for p in range(NH // 2):
                        last = nc.tensor.transpose(bank[g][:, p * T // 2:(p + 1) * T // 2].bitcast(BF16),
                                                   QKS[:, b, g, 2 * p:2 * p + 2, :].rearrange("p h c -> p (h c)"),
                                                   identb[:])
                last.then_inc(S["qkT_mm"], 1)

            def scores_a(b, g):
                i = 4 * b + g
                if i >= 2:
                    pe.wait_ge(S["mx_ready"], i - 1)
                for j in range(2):
                    last = mm(bank[2 + g % 2][:, 2 * j * T:2 * (j + 1) * T], QT[:, b % 2, 2 * g + j, :],
                              KT[:, b % 2, 2 * g + j, :, :].rearrange("p i k -> p (i k)"), start=True, stop=True)
                last.then_inc(S["scoreA"], 1)

            def scores_b(b, g):
                i = 4 * b + g
                if i >= 2:
                    pe.wait_ge(S["pr_ready"], i - 1)
                for j in range(4):
                    pair = 2 * g + j // 2
                    last = mm(bank[4 + g % 2][:, j * T:(j + 1) * T], KT[:, b % 2, pair, j % 2, :],
                              QT[:, b % 2, pair, :], start=True, stop=True)
                last.then_inc(S["scoreB"], 1)

            def weighted(b, g):
                pe.wait_ge(S["pr_ready"], 4 * b + g + 1)
                if b >= 1 and g == 0:
                    pe.wait_ge(S["oT_sb"], b)
                for j in range(4):
                    head = 4 * g + j
                    lo, col = VW * (head % 4), T * (head // 4)
                    last = mm(bank[6][lo:lo + VW, col:col + T], VA[:, b, head, :], PR[:, b % 2, 4 * g + j, :],
                              start=True, stop=True)
                if g == 3:
                    last.then_inc(S["pv_mm"], 1)

            def maxima_transposed(b):
                pe.wait_ge(S["ms_ready"], b + 1)
                if b >= 2:
                    pe.wait_ge(S["x2_ready"], b - 1)
                for p in range(NH // 2):
                    last = nc.tensor.transpose(bank[7][:, p * T // 2:(p + 1) * T // 2].bitcast(BF16),
                                               QKS[:, b, 0, 2 * p:2 * p + 2, :].rearrange("p h c -> p (h c)"),
                                               identb[:])
                last.then_inc(S["mxT_mm"], 1)

            def back(b):
                pe.wait_ge(S["os_sb"], b + 1)
                if b + 1 < B:
                    pe.wait_ge(S["mxT_sb"], b + 2)
                if b >= 1:
                    pe.wait_ge(S["x2_ready"], b)
                for j in range(4):
                    last = nc.tensor.transpose(bank[7][:, j * P:(j + 1) * P], OS[:, j, :], ident)
                last.then_inc(S["back_mm"], 1)

            def out_transposed(b):
                pe.wait_ge(S["o_ready"], b + 1)
                nc.tensor.transpose(bank[6][:, 0:T], OA[:, b % 2, 0:P], ident)
                nc.tensor.transpose(bank[6][0:R, T:2 * T], OA[:, b % 2, P:C], ident).then_inc(S["oT_mm"], 1)

            def projected(b):
                pe.wait_ge(S["oT_sb"], b + 1)
                if b + 1 < B:
                    pe.wait_ge(S["mxT_sb"], b + 2)
                mm(bank[7][:, 0:C], OT_m[:, b % 2, :], wp_m[:], start=True, stop=False)
                mm(bank[7][:, 0:C], OT_r[:, b % 2, :], wp_r[:], start=False, stop=True).then_inc(S["attn_mm"], 1)

            stacks_transposed(0)
            pe.wait_ge(S["qT_sb"], 1)
            pe.wait_ge(S["kT_sb"], 1)
            for g in range(4):
                scores_a(0, g)
            stacks_transposed(1)
            maxima_transposed(0)
            pe.wait_ge(S["qT_sb"], 2)
            pe.wait_ge(S["kT_sb"], 2)
            scores_a(1, 0)
            scores_a(1, 1)
            for b in range(B):
                pe.wait_ge(S["mxT_sb"], b + 1)
                scores_b(b, 0)
                scores_b(b, 1)
                if b >= 1:
                    out_transposed(b - 1)
                if b + 1 < B:
                    scores_a(b + 1, 2)
                if b >= 1:
                    projected(b - 1)
                weighted(b, 0)
                scores_b(b, 2)
                if b + 1 < B:
                    scores_a(b + 1, 3)
                else:
                    transposed(1, 0)
                weighted(b, 1)
                scores_b(b, 3)
                if b + 2 < B:
                    stacks_transposed(b + 2)
                if b + 1 < B:
                    maxima_transposed(b + 1)
                weighted(b, 2)
                weighted(b, 3)
                if b + 2 < B:
                    pe.wait_ge(S["qT_sb"], b + 3)
                    pe.wait_ge(S["kT_sb"], b + 3)
                    scores_a(b + 2, 0)
                    scores_a(b + 2, 1)
                back(b)
            out_transposed(B - 1)
            projected(B - 1)

            def up(h, j):
                n = h * UP + j
                if n >= 3:
                    pe.wait_ge(S["act_ready"], n - 2)
                cols = slice(j * P, (j + 1) * P)
                dst = bank[n % 3][:, :]
                mm(dst, w1_m[:, cols], HT[:, h * HALF:(h + 1) * HALF], start=True, stop=False)
                mm(dst, w1_s[:, cols], HST[:, h * HALF:(h + 1) * HALF], start=False, stop=True)\
                    .then_inc(S["up_mm"], 1)

            def down(b):
                i = b % 4
                if b >= 2:
                    pe.wait_ge(S["down_used"], b - 1)
                for e in range(NE):
                    dst = bank[3 + 2 * (b % 2) + e % 2][:, (e // 2) * C:(e // 2 + 1) * C]
                    first, end = e * HID, (e + 1) * HID
                    for t in range(first // P, -(-end // P)):
                        if i == 0:
                            pe.wait_ge(S["act_ready"], (b // 4) * UP + t + 1)
                        rows = slice(max(first - t * P, 0), min(end - t * P, P))
                        mm(dst, HM[rows, t, i * T:(i + 1) * T], w2_s[rows, t, :],
                           start=(t == first // P), stop=(t == -(-end // P) - 1))
                if b == 0:
                    pe.wait_ge(S["cw_ready"], 1)
                    for h in range(2):
                        for c in range(4):
                            last = nc.tensor.transpose(bank[5 + h][0:NE, c * T:(c + 1) * T], cw[:, 4 * h + c, :],
                                                       ident)
                        last.then_inc(S["cwT_mm"], 1)
                    pe.wait_ge(S["cwT_sb"], 2)
                mm(bank[3 + 2 * (b % 2)][:, 2 * C:3 * C], rt(cwT, b), b2_s[:], start=True, stop=True)\
                    .then_inc(S["down_mm"], 1)

            pe.wait_ge(S["wst_ready"], N_ST // ST_COLS)
            pe.wait_ge(S["mx_ready"], 4 * B)
            pe.wait_ge(S["hT_sb"], 3)
            for j in range(UP_BEFORE_NORM):
                up(0, j)
            transposed(1, 1)
            for j in range(UP_BEFORE_NORM, UP_BEFORE_LOGITS):
                up(0, j)
            pe.wait_ge(S["hT_sb"], 4)
            pe.wait_ge(S["x2_ready"], B)
            for b in range(B):
                dst = bank[7][:, b * NE:(b + 1) * NE]
                mm(dst, rt(HT, b), wg_m, start=True, stop=False)
                last = mm(dst, rt(HST, b), wg_s, start=False, stop=True)
            last.then_inc(S["lg_mm"], 1)
            for j in range(UP_BEFORE_LOGITS, UP):
                up(0, j)
            for b in range(4):
                down(b)
            for j in range(UP):
                up(1, j)
            for b in range(4, B):
                down(b)

        count = [0]

        @block.vector
        def _(dve):
            V = nc.vector

            def start(ins):
                count[0] += 1
                ins.then_inc(dve_done, 1)
                return count[0]

            def seq(ins):
                dve.wait_ge(dve_done, start(ins))

            dve.wait_ge(in_cst, 16)
            V.tensor_copy(identb[:], ident).then_inc(S["identb_ready"], 1)

            def beside_elimination():
                yield from steps(0, 13)
                dve.wait_ge(S["quad_in"], 32)
                dve.wait_ge(S["quad_sb"], 1)
                seq(V.tensor_tensor(A[:], A[:], rot_bias.unsqueeze(1).to_broadcast([P, 4, D]), ALU.add))
                V.tensor_tensor(A[:], A[:], skew_sign.unsqueeze(1).to_broadcast([P, 4, D]), ALU.mult)\
                    .then_inc(S["a_ready"], 1)
                yield from steps(13, 18)
                dve.wait_ge(S["n3_sb"], 4)
                idb = id_stacked.unsqueeze(1).to_broadcast([P, 4, D])
                for n, two in enumerate((((Chi, cosc[4:]), (Dhi, sinc[4:])), ((Clo, cosc[:4]), (Dlo, sinc[:4])))):
                    for power, term in ((2, N2), (1, N1), (0, idb)):
                        for p, c in two:
                            if p is Clo and power == 0:
                                continue
                            ins = V.scalar_tensor_tensor(p, term, c[power], p, ALU.mult, ALU.add)
                            if n == 0 and power == 0:
                                ins.then_inc(S["hi_ready"], 1)
                            else:
                                at = start(ins)
                        if power < 2:
                            yield
                        dve.wait_ge(dve_done, at)
                dve.wait_ge(S["hi_mm"], 1)
                V.tensor_tensor(Clo, bank[5][:, 0:4 * D].rearrange("p (b j) -> p b j", b=4), Clo, ALU.add)\
                    .then_inc(S["cd_ready"], 1)
                V.tensor_tensor(Dlo, bank[5][:, 4 * D:8 * D].rearrange("p (b j) -> p b j", b=4), Dlo, ALU.add)\
                    .then_inc(S["cd_ready"], 1)
                yield
                dve.wait_ge(S["mod_mm"], 1)
                seq(V.tensor_copy(MOD[:], bank[2][:, 0:4 * B].rearrange("p (c b) -> p c b", c=4)))
                sc = MOD[:].rearrange("p (l k) b -> p l k b", l=2)[:, :, 1, :]
                V.tensor_scalar(sc, sc, 1.0, None, ALU.add).then_inc(S["mod_sb"], 1)
                yield
                dve.wait_ge(S["cd_ready"], 2)
                dve.wait_ge(S["ad_mm"], 1)
                ad = bank[6][:, 0:4 * D].rearrange("p (b j) -> p b j", b=4)
                V.tensor_tensor(X[:, 1], ad, Clo, ALU.add).then_inc(S["x_ready"], 1)
                V.scalar_tensor_tensor(X[:, 0], ad, -1.0, Clo, ALU.mult, ALU.add).then_inc(S["x_ready"], 1)
                yield
                dve.wait_ge(S["gate_sb"], 1)
                sc = gates8[:, 2 * C:].rearrange("p (l k c) -> p l k c", l=2, k=3)[:, :, 1, :]
                V.tensor_scalar(sc, sc, 1.0, None, ALU.add).then_inc(S["gates_ready"], 2)
                for n in range(2 * NSQ):
                    yield
                    h = n % 2
                    dve.wait_ge(S["sq_mm"], n + 1)
                    if n < 2 * (NSQ - 1):
                        dve.wait_ge(S["sqi_mm"], n + 1)
                    F = X_diag[:, 0, 2 * h:2 * h + 2, :]
                    V.scalar_tensor_tensor(F, F, 2.0, bank[3 + h][:, 0:2 * P].rearrange("p (b j) -> p b j", b=2),
                                           ALU.mult, ALU.add).then_inc(S["squared"], 1)

            dve.wait_ge(S["gram_ready"], 1)
            V.tensor_scalar(TOP[:], PT[:, 0:D], 0.5, None, ALU.mult).then_inc(S["top_used"], 1)
            seq(V.tensor_copy(EL[:, 0:D], bank[0][0:D, 0:D]))
            V.tensor_copy(EL[:, D:2 * D], id64).then_inc(S["row_used"], 1)

            def pivot(k):
                dve.wait_ge(S["row_ready"], k + 1)
                V.reciprocal(rpiv[:, k % 2:k % 2 + 1], bank[0][0:D, 0:1]).then_inc(S["rpiv_ready"], 1)

            def gram_update(k):
                dve.wait_ge(S["coef_ready"], k + 1)
                if k:
                    dve.wait_ge(S["row_used"], k + 1)
                win = EL[:, k + 1:k + 1 + D]
                V.scalar_tensor_tensor(win, bank[0][0:D, 1:D + 1], coef[:, k % 2:k % 2 + 1], win,
                                       ALU.mult, ALU.add).then_inc(S["row_used"], 1)

            def top_scaled(k):
                dve.wait_ge(S["rnrm_ready"], k + 1)
                dve.wait_ge(S["top_used"], k + 1)
                start(V.tensor_tensor(scaled[:], TOP[:, k:k + 1], rnrm_below[:, k % 2:k % 2 + 1], ALU.mult))

            beside = beside_elimination()
            pivot(0)
            gram_update(0)
            top_scaled(0)
            for k in range(D):
                row = bank[1]
                col = slice(k % 2, k % 2 + 1)
                sign = SG[:, k:k + 1]
                dve.wait_ge(S["top_ready"], k + 1)
                signed = start(V.tensor_scalar(sign, row[0:D, 0:1], 0.0, -0.5, ALU.is_ge, ALU.add))
                if k == D - 1:
                    break
                over_norm = start(V.tensor_tensor(sized[:], row[0:D, 0:1], rnrm[:, col], ALU.mult))
                dve.wait_ge(dve_done, over_norm)
                led = start(V.tensor_tensor(lead[:], sized[:], sign, ALU.add))
                if k + 1 < D - 1:
                    pivot(k + 1)
                start(V.scalar_tensor_tensor(reflected[:], coef[:, col], sign, scaled[:], ALU.mult, ALU.add))
                dve.wait_ge(dve_done, led)
                inverted = start(V.reciprocal(rlead[:], lead[:]))
                dve.wait_ge(dve_done, inverted)
                weighed = start(V.tensor_tensor(tcoef[:], reflected[:], rlead[:], ALU.mult))
                dve.wait_ge(dve_done, weighed)
                V.scalar_tensor_tensor(TOP[:, k + 1:D], row[0:D, 1:D - k], tcoef[:], TOP[:, k + 1:D],
                                       ALU.mult, ALU.add).then_inc(S["top_used"], 1)
                if k + 1 < D - 1:
                    gram_update(k + 1)
                    top_scaled(k + 1)
                    next(beside, None)
                else:
                    dve.wait_ge(S["row_used"], D)
                    seq(V.tensor_tensor(diagonal[:], EL[:, 0:D], id64, ALU.mult))
                    V.tensor_reduce(piv[:], diagonal[:], AX_X, ALU.add).then_inc(S["piv_ready"], 1)
            dve.wait_ge(dve_done, signed)
            seq(V.tensor_tensor(sign_of[:], SG[:], id64, ALU.mult))
            seq(V.tensor_reduce(sigma[:], sign_of[:], AX_X, ALU.add))
            dve.wait_ge(S["rnorm_ready"], 1)
            seq(V.tensor_scalar(signed_rnorm[:], sigma[:], 2.0, rnorm[:], ALU.mult, ALU.mult))
            V.tensor_scalar(LN[:], EL[:, D:2 * D], signed_rnorm[:], None, ALU.mult).then_inc(S["ln_ready"], 1)
            next(beside, None)
            dve.wait_ge(S["linvT_ready"], 1)
            V.tensor_copy(LT[:], bank[0][0:D, 0:D]).then_inc(S["lT_ready"], 1)
            next(beside, None)
            dve.wait_ge(S["z_ready"], 2)
            V.tensor_copy(Z0T[:], bank[2][:, :]).then_inc(S["z_sb"], 1)
            dve.wait_ge(S["basis_ready"], 1)
            V.tensor_copy(U0T[:], bank[1][0:D, 0:C]).then_inc(S["z_sb"], 1)
            for _ in beside:
                pass
            dve.wait_ge(S["turn_ready"], 1)
            V.tensor_copy(WT[:, 0:HALF], bank[4][0:D, :]).then_inc(S["turned_ready"], 1)

            def norm_stats(src, ln, b):
                seq(V.bn_stats(stats[:, b, :], src))
                V.bn_aggr(mv[:, ln, b, :], stats[:, b, :]).then_inc(S["var_ready"], 1)

            def normalized(src, ln, h):
                u = 2 * ln + h
                dve.wait_ge(S["var_ready"], 4 * (u + 1))
                dve.wait_ge(S["rstd_ready"], u + 1)
                half = slice(4 * h, 4 * h + 4)
                for b in range(4 * h, 4 * h + 4):
                    ins = V.tensor_scalar(H[:, b, :], src[:, b, :], mv[:, ln, b, 0:1], rstd[:, ln, b:b + 1],
                                          ALU.subtract, ALU.mult)
                ins.then_inc(S["h_ready"], 1)
                dve.wait_ge(S["h_ready"], u + 1)
                stack = HS[:, half, 0:RS].rearrange("p b (s c) -> p b s c", s=SLOTS)
                seq(V.tensor_tensor(hr[:], H[:, half, P:C], MB[:, half, 3 * ln + 1, :], ALU.mult))
                seq(V.tensor_tensor(hr[:], hr[:], MB[:, half, 3 * ln, :], ALU.add))
                seq(V.tensor_copy(stack[:, :, 0:3, :], hr[:].unsqueeze(2).to_broadcast([P, 4, 3, R])))
                seq(V.tensor_tensor(hres[:], hr[:], stack[:, :, 0, :], ALU.subtract))
                seq(V.tensor_copy(stack[:, :, 3:6:2, :], hres[:].unsqueeze(2).to_broadcast([P, 4, 2, R])))
                seq(V.tensor_tensor(hr[:], hres[:], stack[:, :, 3, :], ALU.subtract))
                V.tensor_copy(stack[:, :, 4, :], hr[:]).then_inc(S["hs_ready"], 1)
                dve.wait_ge(S["hs_ready"], u + 1)

            def moved(b):
                dve.wait_ge(S["delta_ready"], b + 1)
                V.tensor_tensor(XR[:, b, :], bank[b % 2][:, 0:C], x_in[:, b, :], ALU.add).then_inc(S["xr_used"], 1)
                dve.wait_ge(S["xr_used"], b + 1)
                norm_stats(XR[:, b, :], 0, b)

            for b in range(4):
                moved(b)
            dve.wait_ge(S["zeroed"], 6)
            dve.wait_ge(gates_in, 32)
            moved(4)
            normalized(XR, 0, 0)
            for b in range(5, B):
                moved(b)
            normalized(XR, 0, 1)
            for b in range(B):
                dve.wait_ge(S["qk1_sb"], b + 1)
                qkv = bank[4 + b % 4]
                V.tensor_copy(VA[:, b, :, 0:HD], qkv[:, 2 * C:3 * C].rearrange("p (h d) -> p h d", h=NH))
                V.tensor_tensor(qkres[:, b, :].rearrange("p (g d) -> p g d", d=HD),
                                qkv[:, 0:2 * C].rearrange("p (g d) -> p g d", d=HD),
                                QKS[:, b, :, :, 2 * HD:3 * HD].rearrange("p g h d -> p (g h) d"), ALU.subtract)\
                    .then_inc(S["r1_ready"], 1)

            def stacks_moved(b):
                dve.wait_ge(S["qkT_mm"], b + 1)
                if b >= 2:
                    dve.wait_ge(S["scoreB"], 4 * b - 4)
                for i in range(2):
                    half = slice(i * HK, (i + 1) * HK)
                    ins = V.tensor_copy(KT[half, b % 2, :, i, :],
                                        bank[1][half, :].bitcast(BF16).rearrange("p (h k) -> p h k", h=NH // 2))
                ins.then_inc(S["kT_sb"], 1)

            def maxima(b, groups):
                for g in groups:
                    dve.wait_ge(S["scoreA"], 4 * b + g + 1)
                    V.tensor_reduce(nmax[:, 4 * g:4 * g + 4],
                                    bank[2 + g % 2][:, :].rearrange("p (h k) -> p h k", h=4), AX_X, ALU.max, negate=True).then_inc(S["mx_ready"], 1)

            def maxima_stacked(b):
                dve.wait_ge(S["mx_ready"], 4 * b + 4)
                parts = QKS[:, b, 0, :, DK:DM]
                seq(V.tensor_copy(parts[:, :, 0], nmax[:]))
                seq(V.tensor_tensor(nmres[:], nmax[:], parts[:, :, 0], ALU.subtract))
                V.tensor_copy(parts[:, :, 1], nmres[:]).then_inc(S["ms_ready"], 1)
                dve.wait_ge(S["ms_ready"], b + 1)

            def divided(b):
                dve.wait_ge(S["back_mm"], b + 1)
                o = bank[7][:, :].rearrange("p (h d) -> p h d", h=NH)
                seq(V.reciprocal(rsum[:, b % 2, :], o[:, :, HD]))
                V.tensor_tensor(OA[:, b % 2, :].rearrange("p (h d) -> p h d", h=NH), o[:, :, 0:HD],
                                rsum[:, b % 2, :].unsqueeze(2).to_broadcast([P, NH, HD]), ALU.mult)\
                    .then_inc(S["o_ready"], 1)

            def added(b):
                dve.wait_ge(S["attn_mm"], b + 1)
                seq(V.tensor_tensor(PG[:, b % 2, :], bank[7][:, 0:C], GB[:, b, 0, :], ALU.mult))
                V.tensor_tensor(X2[:, b, :], PG[:, b % 2, :], XR[:, b, :], ALU.add).then_inc(S["x2_ready"], 1)

            def summed(b):
                dve.wait_ge(S["x2_ready"], b + 1)
                norm_stats(X2[:, b, :], 1, b)

            stacks_moved(0)
            maxima(0, range(4))
            maxima_stacked(0)
            stacks_moved(1)
            maxima(1, (0, 1))
            for b in range(B):
                if b + 1 < B:
                    maxima(b + 1, (2, 3))
                    maxima_stacked(b + 1)
                if b >= 1:
                    added(b - 1)
                if b + 2 < B:
                    stacks_moved(b + 2)
                if b >= 1:
                    summed(b - 1)
                if b + 2 < B:
                    maxima(b + 2, (0, 1))
                divided(b)
                if b == B - 2:
                    normalized(X2, 1, 0)
            added(B - 1)
            summed(B - 1)
            normalized(X2, 1, 1)

            dve.wait_ge(S["lg_sb"], 1)
            other = lg[:].unsqueeze(2).to_broadcast([P, B, NE, NE])
            own = lg[:].unsqueeze(3).to_broadcast([P, B, NE, NE])
            seq(V.tensor_tensor(gt[:], other, own, ALU.is_gt))
            seq(V.tensor_tensor(eq[:], other, own, ALU.is_equal))
            ties = rank_ties.unsqueeze(1).to_broadcast([P, B, NE * NE])
            eqf = eq[:].rearrange("p b e f -> p b (e f)")
            seq(V.tensor_tensor(eqf, eqf, ties, ALU.mult))
            seq(V.tensor_tensor(gt[:], gt[:], eq[:], ALU.add))
            seq(V.tensor_reduce(rank[:], gt[:], AX_X, ALU.add))
            seq(V.tensor_scalar(rank[:], rank[:], 1.5, None, ALU.is_lt))
            seq(V.tensor_reduce(gmax[:], lg[:], AX_X, ALU.max))
            V.tensor_tensor(sel[:], lg[:], gmax[:].unsqueeze(2).to_broadcast([P, B, NE]), ALU.subtract)\
                .then_inc(S["sel_ready"], 1)
            dve.wait_ge(S["exp_ready"], 1)
            seq(V.tensor_tensor(sel[:], sel[:], rank[:], ALU.mult))
            seq(V.tensor_reduce(gsum[:], sel[:], AX_X, ALU.add))
            seq(V.reciprocal(rgs[:], gsum[:]))
            V.tensor_tensor(cw[:], sel[:], rgs[:].unsqueeze(2).to_broadcast([P, B, NE]), ALU.mult)\
                .then_inc(S["cw_ready"], 1)
            dve.wait_ge(S["cw_ready"], 1)
            for b in range(B):
                acc = ACC[:, b % 2, :]
                dve.wait_ge(S["down_mm"], b + 1)
                lo = 3 + 2 * (b % 2)
                seq(V.tensor_copy(acc, bank[lo][:, 2 * C:3 * C]))
                for e in range(NE):
                    src = bank[lo + e % 2][:, (e // 2) * C:(e // 2 + 1) * C]
                    ins = V.scalar_tensor_tensor(acc, src, cw[:, b, e:e + 1], acc, ALU.mult, ALU.add)
                    if e == NE - 1:
                        ins.then_inc(S["down_used"], 1)
                        dve.wait_ge(S["down_used"], b + 1)
                    else:
                        seq(ins)
                seq(V.tensor_tensor(acc, acc, GB[:, b, 1, :], ALU.mult))
                V.tensor_tensor(X2[:, b, :], acc, X2[:, b, :], ALU.add).then_inc(S["res_ready"], 1)


def _layout(inputs):
    import numpy as np
    f = {k: np.asarray(v) for k, v in inputs.items()}
    ones = lambda n: np.ones((1, n), np.float32)

    def with_bias(w, b):
        return np.ascontiguousarray(np.concatenate([w, b.reshape(1, -1)], 0))

    x = np.ascontiguousarray(f["x"])
    iu, ju = np.triu_indices(D, k=1)
    rot = np.zeros((C, D, D), np.float32)
    rot[:, ju, iu] = f["L0_cond_W"].T
    rot[:, iu, ju] = f["L0_cond_W"].T
    rot = rot.reshape(C, 2, D // 2, D).transpose(0, 2, 1, 3)
    cond_diag = np.zeros((8, R, 8, B), np.float32)
    for j in range(8):
        cond_diag[j, :, j] = f["cond_1152"].T[P:]
    cond_diag = cond_diag.reshape(P, 8 * B)
    rot_last = rot[P:].reshape(R, 4, 8, P).transpose(2, 0, 1, 3)
    bias_of = np.zeros((D, D), np.float32)
    bias_of[ju, iu] = f["L0_cond_b"]
    bias_of[iu, ju] = f["L0_cond_b"]
    qkv, w1 = f["L1_cond_w_qkv"], f["L1_cond_w1"].transpose(1, 0, 2).reshape(C, NE * HID)
    main = np.concatenate([qkv, f["L1_cond_w_gate"], w1], 1)
    bias = np.concatenate([f["L1_cond_b_qkv"], np.zeros(NE, np.float32), f["L1_cond_b1"].reshape(-1)])
    stack = np.concatenate([np.tile(main[P:C], (SLOTS, 1)), np.tile(bias[None], (3, 1))], 0)
    rows_of = np.repeat(np.array(WPART), R).tolist() + [1, 2, 3]
    c = np.zeros((P, 648), np.float32)
    c[:, 0:P] = np.eye(P)
    i = np.arange(D)
    c[0:D, 192:256] = -(i[:, None] > i[None, :]).astype(np.float32)
    c[:, 256:320] = np.tile(np.sign(i[None, :] - i[:, None]), (2, 1)) * 2.0 ** -NSQ
    c[:, 520:648] = 2.0 * np.eye(P)
    c[:, 392:456] = np.tile(np.eye(D), (2, 1))
    c[:, 456:520] = np.tile(bias_of, (2, 1))
    e = np.arange(NE)
    c[:, 360:376] = (e[None, :] < e[:, None]).astype(np.float32).reshape(1, NE * NE)
    c[0:RK, 380] = [-1.0 if r >= 2 else 0.0 for r in rows_of]
    c[0:RK, 381] = [-1.0 if r == 3 else 0.0 for r in rows_of]
    return {
        "xtok": x, "xT": np.ascontiguousarray(x.reshape(B * T, C).T),
        "pmat": f["L0_cond_P"], "pT": np.ascontiguousarray(f["L0_cond_P"].T),
        "condT": np.concatenate([f["cond_1152"].T, ones(B)], 0),
        "rotW": rot[0:P].reshape(P, D * D), "condR": cond_diag, "rotR": rot_last.reshape(P, 4 * P),
        "adaW": with_bias(f["L1_cond_w_adaln"], f["L1_cond_b_adaln"]),
        "wproj": with_bias(f["L1_cond_w_proj"], f["L1_cond_b_proj"]),
        "wmain": main[0:P], "wstack": stack,
        "w2": f["L1_cond_w2"].reshape(NE * HID, C), "b2": f["L1_cond_b2"], "consts": c,
    }


def kernel(**inputs):
    import numpy as _np
    import concourse.bacc as _bacc
    from concourse import mybir as _mybir
    from concourse.bass_utils import run_bass_kernel_spmd as _run

    nc = _bacc.Bacc("TRN2", target_bir_lowering=False, num_devices=1)
    arrays, args = {}, {}
    for name, a in _layout(inputs).items():
        a = _np.ascontiguousarray(a)
        arrays[f"in_{name}"] = a
        args[name] = nc.dram_tensor(f"in_{name}", a.shape, _mybir.dt.from_np(a.dtype), kind="ExternalInput").ap()
    out = nc.dram_tensor("out", (B, T, C), _mybir.dt.from_np(_np.dtype("float32")), kind="ExternalOutput").ap()
    bass_conditional_rotation_moe_block(nc, out=out, **args)
    r = _run(nc, [arrays], core_ids=[0])
    return r.results[0]["out"]
```
